# Optimizing a Trainium2 kernel written in Bass

```python
import numpy as np
import jax
import jax.numpy as jnp

def _softmax(x, axis=-1):
    return jax.nn.softmax(x, axis=axis)

def _gelu(x):
    return jax.nn.gelu(x, approximate=True)

def _silu(x):
    return jax.nn.silu(x)

def _sigmoid(x):
    return jax.nn.sigmoid(x)

def _layernorm(x, axis=-1, eps=1e-05):
    m = jnp.mean(x, axis=axis, keepdims=True)
    v = jnp.var(x, axis=axis, keepdims=True)
    return (x - m) / jnp.sqrt(v + eps)

def _scatter_add(tgt, idx, src, axis=0):
    return tgt.at[idx].add(src)

def _segment_sum(src, seg, n):
    return jax.ops.segment_sum(src, seg, n)
kernel_name = 'mk_xattn_seq_d2_seqx_r4_293345'

def setup_inputs(seed: int=0):
    np.random.seed(seed)
    _w = jnp.asarray

    def _rec_inputs():
        import jax
        import jax.numpy as jnp
        _rk = jax.random.key(seed)
        x = -0.0002928 + 1 * jax.random.normal(jax.random.fold_in(_rk, 1), (16, 256, 256), jnp.float32)
        _lenS = 256 - jax.random.randint(jax.random.fold_in(_rk, 7), (16,), 0, max(1, 256 // 4) + 1, jnp.int32)
        _lenS2 = 256 - jax.random.randint(jax.random.fold_in(_rk, 8), (16,), 0, max(1, 256 // 4) + 1, jnp.int32)
        _ctx_1024P = jax.random.normal(jax.random.fold_in(_rk, 11), (16, 16, 256), jnp.float32)
        _ctx_1024c = jax.random.dirichlet(jax.random.fold_in(_rk, 511), 0.3 * jnp.ones((16,), jnp.float32), (16, 256))
        _ctx_1024t = jnp.einsum('bsk,bkd->bsd', _ctx_1024c, _ctx_1024P)
        _ctx_1024t = _ctx_1024t * jax.lax.rsqrt(jnp.mean(jnp.square(_ctx_1024t)) + 1e-12) * 0.953939
        ctx_1024 = -1.39393e-06 + 0.999914 * (_ctx_1024t + 0.3 * jax.random.normal(jax.random.fold_in(_rk, 611), (16, 256, 256), jnp.float32))
        _validS = jnp.arange(256)[None, :] < _lenS[:, None]
        _validS2 = jnp.arange(256)[None, :] < _lenS2[:, None]
        _causal = jnp.tril(jnp.ones((256, 256), dtype=bool))
        mask_BxSxS2_bf0 = jnp.logical_not(jnp.ones((16, 256, 256), dtype=bool))
        mask_SxS_ik1 = jnp.where(jnp.broadcast_to(_validS[0:1, :], (256, 256)), 1, 0).astype(jnp.int32)
        return (x, ctx_1024, mask_BxSxS2_bf0, mask_SxS_ik1)
    x, ctx_1024, mask_BxSxS2_bf0, mask_SxS_ik1 = _rec_inputs()

    def _L0_xattn_setup():
        import jax, jax.numpy as jnp
        import numpy as np
        B, S, D_MODEL, H, DH = (2, 512, 256, 16, 64)
        LN_EPS = 1e-05
        key = jax.random.key(seed)
        ks = jax.random.split(key, 12)
        sc_in = 1.0 / np.sqrt(D_MODEL)
        sc_hd = 1.0 / np.sqrt(H * DH)
        return {'Q': jax.random.normal(ks[0], (B, S, D_MODEL), jnp.float32), 'K': jax.random.normal(ks[1], (B, S, D_MODEL), jnp.float32), 'V': jax.random.normal(ks[2], (B, S, D_MODEL), jnp.float32), 'attn_mask': jnp.zeros((B, S, S), dtype=bool), 'Wq': jax.random.normal(ks[3], (D_MODEL, H * DH), jnp.float32) * sc_in, 'bq': jax.random.normal(ks[4], (H * DH,), jnp.float32) * 0.01, 'Wk': jax.random.normal(ks[5], (D_MODEL, H * DH), jnp.float32) * sc_in, 'bk': jax.random.normal(ks[6], (H * DH,), jnp.float32) * 0.01, 'Wv': jax.random.normal(ks[7], (D_MODEL, H * DH), jnp.float32) * sc_in, 'bv': jax.random.normal(ks[8], (H * DH,), jnp.float32) * 0.01, 'Wo': jax.random.normal(ks[9], (H * DH, D_MODEL), jnp.float32) * sc_hd, 'bo': jax.random.normal(ks[10], (D_MODEL,), jnp.float32) * 0.01, 'gamma': jnp.ones((D_MODEL,), jnp.float32), 'beta': jnp.zeros((D_MODEL,), jnp.float32)}
    _L0_xattn_all = _L0_xattn_setup()
    _L0_xattn_in = {k: v for k, v in _L0_xattn_all.items() if k in ('Wq', 'bq', 'Wk', 'bk', 'Wv', 'bv', 'Wo', 'bo', 'gamma', 'beta')}
    del _L0_xattn_all

    def _L1_xattn_setup():
        import jax, jax.numpy as jnp
        import numpy as np
        D_MODEL = 256
        N_HEAD = 16
        D_FF = 1024
        EPS = 1e-05

        def _linear(x, w, b):
            return jnp.einsum('bli,io->blo', x, w) + b

        def _layernorm(x, g, b):
            mu = jnp.mean(x, -1, keepdims=True)
            var = jnp.mean(jnp.square(x - mu), -1, keepdims=True)
            return (x - mu) * jax.lax.rsqrt(var + EPS) * g + b

        def _attention(q, k, v, mask):
            B, Lq, D = q.shape
            H = N_HEAD
            hd = D // H
            qh = q.reshape(B, Lq, H, hd)
            kh = k.reshape(B, k.shape[1], H, hd)
            vh = v.reshape(B, v.shape[1], H, hd)
            scores = jnp.einsum('bqhd,bkhd->bhqk', qh, kh) / jnp.sqrt(jnp.float32(hd)).astype(q.dtype)
            if mask is not None:
                scores = jnp.where(mask[None, None] != 0, jnp.finfo(scores.dtype).min, scores)
            p = jax.nn.softmax(scores, axis=-1)
            out = jnp.einsum('bhqk,bkhd->bqhd', p, vh).reshape(B, Lq, D)
            return out
        key = jax.random.key(seed)
        ks = jax.random.split(key, 32)
        B, L, S, D, F = (2, 512, 512, D_MODEL, D_FF)
        std = 0.02
        inp = {'tgt': jax.random.normal(ks[0], (B, L, D), jnp.float32), 'memory': jax.random.normal(ks[1], (B, S, D), jnp.float32), 'tgt_mask': jnp.triu(jnp.ones((L, L), jnp.int32), k=1)}
        names = ['q', 'k', 'v', 'o', 'cq', 'ck', 'cv', 'co']
        for i, n in enumerate(names):
            inp[n + '_w'] = jax.random.normal(ks[2 + i], (D, D), jnp.float32) * std
            inp[n + '_b'] = jnp.zeros((D,), jnp.float32)
        inp['lin1_w'] = jax.random.normal(ks[12], (D, F), jnp.float32) * std
        inp['lin1_b'] = jnp.zeros((F,), jnp.float32)
        inp['lin2_w'] = jax.random.normal(ks[13], (F, D), jnp.float32) * std
        inp['lin2_b'] = jnp.zeros((D,), jnp.float32)
        for i, n in enumerate(['ln1', 'ln2', 'ln3']):
            inp[n + '_g'] = jnp.ones((D,), jnp.float32)
            inp[n + '_b'] = jnp.zeros((D,), jnp.float32)
        return inp
    _L1_xattn_all = _L1_xattn_setup()
    _L1_xattn_in = {k: v for k, v in _L1_xattn_all.items() if k in ('q_w', 'q_b', 'k_w', 'k_b', 'v_w', 'v_b', 'o_w', 'o_b', 'cq_w', 'cq_b', 'ck_w', 'ck_b', 'cv_w', 'cv_b', 'co_w', 'co_b', 'lin1_w', 'lin1_b', 'lin2_w', 'lin2_b', 'ln1_g', 'ln1_b', 'ln2_g', 'ln2_b', 'ln3_g', 'ln3_b')}
    del _L1_xattn_all
    return {'x': x, 'ctx_1024': ctx_1024, 'mask_BxSxS2_bf0': mask_BxSxS2_bf0, 'mask_SxS_ik1': mask_SxS_ik1, 'L0_xattn_Wq': _L0_xattn_in['Wq'], 'L0_xattn_bq': _L0_xattn_in['bq'], 'L0_xattn_Wk': _L0_xattn_in['Wk'], 'L0_xattn_bk': _L0_xattn_in['bk'], 'L0_xattn_Wv': _L0_xattn_in['Wv'], 'L0_xattn_bv': _L0_xattn_in['bv'], 'L0_xattn_Wo': _L0_xattn_in['Wo'], 'L0_xattn_bo': _L0_xattn_in['bo'], 'L0_xattn_gamma': _L0_xattn_in['gamma'], 'L0_xattn_beta': _L0_xattn_in['beta'], 'L1_xattn_q_w': _L1_xattn_in['q_w'], 'L1_xattn_q_b': _L1_xattn_in['q_b'], 'L1_xattn_k_w': _L1_xattn_in['k_w'], 'L1_xattn_k_b': _L1_xattn_in['k_b'], 'L1_xattn_v_w': _L1_xattn_in['v_w'], 'L1_xattn_v_b': _L1_xattn_in['v_b'], 'L1_xattn_o_w': _L1_xattn_in['o_w'], 'L1_xattn_o_b': _L1_xattn_in['o_b'], 'L1_xattn_cq_w': _L1_xattn_in['cq_w'], 'L1_xattn_cq_b': _L1_xattn_in['cq_b'], 'L1_xattn_ck_w': _L1_xattn_in['ck_w'], 'L1_xattn_ck_b': _L1_xattn_in['ck_b'], 'L1_xattn_cv_w': _L1_xattn_in['cv_w'], 'L1_xattn_cv_b': _L1_xattn_in['cv_b'], 'L1_xattn_co_w': _L1_xattn_in['co_w'], 'L1_xattn_co_b': _L1_xattn_in['co_b'], 'L1_xattn_lin1_w': _L1_xattn_in['lin1_w'], 'L1_xattn_lin1_b': _L1_xattn_in['lin1_b'], 'L1_xattn_lin2_w': _L1_xattn_in['lin2_w'], 'L1_xattn_lin2_b': _L1_xattn_in['lin2_b'], 'L1_xattn_ln1_g': _L1_xattn_in['ln1_g'], 'L1_xattn_ln1_b': _L1_xattn_in['ln1_b'], 'L1_xattn_ln2_g': _L1_xattn_in['ln2_g'], 'L1_xattn_ln2_b': _L1_xattn_in['ln2_b'], 'L1_xattn_ln3_g': _L1_xattn_in['ln3_g'], 'L1_xattn_ln3_b': _L1_xattn_in['ln3_b']}

def reference(x, ctx_1024, mask_BxSxS2_bf0, mask_SxS_ik1, L0_xattn_Wq, L0_xattn_bq, L0_xattn_Wk, L0_xattn_bk, L0_xattn_Wv, L0_xattn_bv, L0_xattn_Wo, L0_xattn_bo, L0_xattn_gamma, L0_xattn_beta, L1_xattn_q_w, L1_xattn_q_b, L1_xattn_k_w, L1_xattn_k_b, L1_xattn_v_w, L1_xattn_v_b, L1_xattn_o_w, L1_xattn_o_b, L1_xattn_cq_w, L1_xattn_cq_b, L1_xattn_ck_w, L1_xattn_ck_b, L1_xattn_cv_w, L1_xattn_cv_b, L1_xattn_co_w, L1_xattn_co_b, L1_xattn_lin1_w, L1_xattn_lin1_b, L1_xattn_lin2_w, L1_xattn_lin2_b, L1_xattn_ln1_g, L1_xattn_ln1_b, L1_xattn_ln2_g, L1_xattn_ln2_b, L1_xattn_ln3_g, L1_xattn_ln3_b):
    import jax
    import jax.numpy as jnp

    def _L0_xattn_ref(Q, K, V, attn_mask, Wq, bq, Wk, bk, Wv, bv, Wo, bo, gamma, beta):
        import jax, jax.numpy as jnp
        import numpy as np
        B, S, D_MODEL, H, DH = (2, 512, 256, 16, 64)
        LN_EPS = 1e-05
        b, s, _ = Q.shape
        q = (Q @ Wq + bq).reshape(b, s, H, DH).transpose(0, 2, 1, 3)
        k = (K @ Wk + bk).reshape(b, s, H, DH).transpose(0, 2, 1, 3)
        v = (V @ Wv + bv).reshape(b, s, H, DH).transpose(0, 2, 1, 3)
        scale = 1.0 / jnp.sqrt(jnp.asarray(DH, q.dtype))
        scores = jnp.einsum('bhqd,bhkd->bhqk', q, k) * scale
        scores = jnp.where(attn_mask[:, None, :, :], jnp.asarray(-1000000000.0, scores.dtype), scores)
        attn = jax.nn.softmax(scores, axis=-1)
        ctx = jnp.einsum('bhqk,bhkd->bhqd', attn, v)
        ctx = ctx.transpose(0, 2, 1, 3).reshape(b, s, H * DH)
        out = ctx @ Wo + bo + Q
        mu = jnp.mean(out, axis=-1, keepdims=True)
        var = jnp.var(out, axis=-1, keepdims=True)
        return (out - mu) * jax.lax.rsqrt(var + LN_EPS) * gamma + beta

    def _L1_xattn_ref(tgt, memory, tgt_mask, q_w, q_b, k_w, k_b, v_w, v_b, o_w, o_b, cq_w, cq_b, ck_w, ck_b, cv_w, cv_b, co_w, co_b, lin1_w, lin1_b, lin2_w, lin2_b, ln1_g, ln1_b, ln2_g, ln2_b, ln3_g, ln3_b):
        import jax, jax.numpy as jnp
        import numpy as np
        D_MODEL = 256
        N_HEAD = 16
        D_FF = 1024
        EPS = 1e-05

        def _linear(x, w, b):
            return jnp.einsum('bli,io->blo', x, w) + b

        def _layernorm(x, g, b):
            mu = jnp.mean(x, -1, keepdims=True)
            var = jnp.mean(jnp.square(x - mu), -1, keepdims=True)
            return (x - mu) * jax.lax.rsqrt(var + EPS) * g + b

        def _attention(q, k, v, mask):
            B, Lq, D = q.shape
            H = N_HEAD
            hd = D // H
            qh = q.reshape(B, Lq, H, hd)
            kh = k.reshape(B, k.shape[1], H, hd)
            vh = v.reshape(B, v.shape[1], H, hd)
            scores = jnp.einsum('bqhd,bkhd->bhqk', qh, kh) / jnp.sqrt(jnp.float32(hd)).astype(q.dtype)
            if mask is not None:
                scores = jnp.where(mask[None, None] != 0, jnp.finfo(scores.dtype).min, scores)
            p = jax.nn.softmax(scores, axis=-1)
            out = jnp.einsum('bhqk,bkhd->bqhd', p, vh).reshape(B, Lq, D)
            return out
        q = _linear(tgt, q_w, q_b)
        k = _linear(tgt, k_w, k_b)
        v = _linear(tgt, v_w, v_b)
        tgt2 = _linear(_attention(q, k, v, tgt_mask), o_w, o_b)
        x = _layernorm(tgt + tgt2, ln1_g, ln1_b)
        q = _linear(x, cq_w, cq_b)
        k = _linear(memory, ck_w, ck_b)
        v = _linear(memory, cv_w, cv_b)
        tgt2 = _linear(_attention(q, k, v, None), co_w, co_b)
        x = _layernorm(x + tgt2, ln2_g, ln2_b)
        tgt2 = _linear(jax.nn.relu(_linear(x, lin1_w, lin1_b)), lin2_w, lin2_b)
        x = _layernorm(x + tgt2, ln3_g, ln3_b)
        return x
    x = _L0_xattn_ref(x, ctx_1024, ctx_1024, mask_BxSxS2_bf0, L0_xattn_Wq, L0_xattn_bq, L0_xattn_Wk, L0_xattn_bk, L0_xattn_Wv, L0_xattn_bv, L0_xattn_Wo, L0_xattn_bo, L0_xattn_gamma, L0_xattn_beta)
    x = _L1_xattn_ref(x, ctx_1024, mask_SxS_ik1, L1_xattn_q_w, L1_xattn_q_b, L1_xattn_k_w, L1_xattn_k_b, L1_xattn_v_w, L1_xattn_v_b, L1_xattn_o_w, L1_xattn_o_b, L1_xattn_cq_w, L1_xattn_cq_b, L1_xattn_ck_w, L1_xattn_ck_b, L1_xattn_cv_w, L1_xattn_cv_b, L1_xattn_co_w, L1_xattn_co_b, L1_xattn_lin1_w, L1_xattn_lin1_b, L1_xattn_lin2_w, L1_xattn_lin2_b, L1_xattn_ln1_g, L1_xattn_ln1_b, L1_xattn_ln2_g, L1_xattn_ln2_b, L1_xattn_ln3_g, L1_xattn_ln3_b)
    return x

_drawn_inputs = setup_inputs


def setup_inputs(seed=0):
    import zlib

    import numpy as np

    out = dict(_drawn_inputs(seed))
    spreads = {'L0_xattn_gamma': (1.0, 0.2),
     'L0_xattn_beta': (0.0, 0.1),
     'L1_xattn_q_b': (0.0, 0.8),
     'L1_xattn_k_b': (0.0, 2.0),
     'L1_xattn_v_b': (0.0, 0.292),
     'L1_xattn_o_b': (0.0, 0.1),
     'L1_xattn_cq_b': (0.0, 0.8),
     'L1_xattn_ck_b': (0.0, 2.0),
     'L1_xattn_cv_b': (0.0, 0.276),
     'L1_xattn_co_b': (0.0, 0.1),
     'L1_xattn_lin1_b': (0.0, 0.1),
     'L1_xattn_lin2_b': (0.0, 0.1),
     'L1_xattn_ln1_g': (1.0, 0.2),
     'L1_xattn_ln1_b': (0.0, 0.1),
     'L1_xattn_ln2_g': (1.0, 0.2),
     'L1_xattn_ln2_b': (0.0, 0.1),
     'L1_xattn_ln3_g': (1.0, 0.2),
     'L1_xattn_ln3_b': (0.0, 0.1)}
    factors = {'L0_xattn_bq': 30.428,
     'L0_xattn_bk': 64.0,
     'L0_xattn_bv': 7.418,
     'L0_xattn_bo': 6.301,
     'L1_xattn_q_w': 8.0,
     'L1_xattn_k_w': 8.0,
     'L1_xattn_cq_w': 8.0,
     'L1_xattn_ck_w': 8.0}
    for name, (base, spread) in spreads.items():
        noise = np.random.default_rng([zlib.crc32(name.encode()), seed]).standard_normal(out[name].shape)
        drawn = base * np.exp(spread * noise) if base else spread * noise
        out[name] = jnp.asarray(drawn.astype(out[name].dtype))
    for name, factor in factors.items():
        out[name] = (out[name] * factor).astype(out[name].dtype)
    return out
```

```python
from contextlib import ExitStack

import numpy as np

import concourse.bass as bass
from concourse import mybir

ALU = mybir.AluOpType
ACT = mybir.ActivationFunctionType
F32 = mybir.dt.float32
BF16 = mybir.dt.bfloat16
I32 = mybir.dt.int32
U8 = mybir.dt.uint8

P = 128
BATCH, TOK, D = 16, 256, 256
TT, DT = TOK // P, D // P
HEADS = 16
PAIRS, QUADS = HEADS // 2, HEADS // 4
DH0, DH1 = 64, D // HEADS
INNER = HEADS * DH0
FF = 1024
SLOT = 32
EPS = 1e-5
BIG = 2.0 ** 127
SCALE = {"A": DH0 ** -0.5, "B": DH1 ** -0.5, "C": DH1 ** -0.5}

P_RING, PT_RING = 4, 3
LAG_R, LAG_T = 1, 2

DVE_JOBS = {"q": 4, "v": 4, "vc": 1, "wo": 1, "qs": 1, "vs": 1, "os": 1, "qc": 1, "oc": 1, "y": 1}
ACT_JOBS = {"xT": 1, "cT": 1, "k": 4, "kc": 1, "x1T": 1, "ks": 1, "x2T": 1, "x3T": 1, "h": 4}
STREAM_A = {"A", "q", "v", "vc", "wo", "xT", "cT", "k", "kc", "ln0"}


def schedule(a, b):
    job = lambda name, i=0: ("J", name, i)
    qkv = [job(n, i) for i in range(4) for n in ("q", "k", "v")]
    pre, order, after = [], [], {}

    def put(key, *steps):
        after.setdefault(key, []).extend(steps)

    if a:
        pre += [job("xT"), job("cT")] + (qkv[:4] if b else qkv)
    if b:
        pre += [job("x1T"), job("qs"), job("ks"), job("vs")]
    quad = lambda n, i: [(n, 2 * i), (n, 2 * i + 1)]
    if a and b:
        order = sum((quad("B", i) for i in range(4)), [])
        order += quad("A", 0) + quad("A", 1)
        order += quad("C", 0) + quad("C", 1) + quad("A", 2) + quad("C", 2) + quad("C", 3) + quad("A", 3)
        for i, step in enumerate(qkv[4:]):
            put(("S", "B", i), step)
    elif a:
        order = sum((quad("A", i) for i in range(4)), [])
    else:
        order = sum((quad("B", i) for i in range(4)), []) + sum((quad("C", i) for i in range(4)), [])

    steps = list(pre)
    tail_b = {"B": [job("os"), ("LN", "ln1", 0), job("x2T"), job("qc")],
              "C": [job("oc"), ("LN", "ln2", 0), job("x3T"), job("h", 0), job("h", 1), job("h", 2),
                    job("h", 3), job("y"), ("LN", "ln3", 0)]}

    def attend(order):
        n = len(order)
        waiting, pending = [], []
        for g in range(n + LAG_T + 1):
            if g < n:
                if order[g] == ("C", 0):
                    steps.extend(pending)
                    pending = []
                steps.append(("S",) + order[g])
                steps.extend(after.get(("S",) + order[g], []))
            for t in waiting:
                steps.append(t)
                if t[2] == QUADS - 1 and t[1] in tail_b:
                    pending += tail_b[t[1]]
            waiting = []
            if pending:
                steps.append(pending.pop(0))
            if 0 <= g - LAG_R < n:
                steps.append(("R",) + order[g - LAG_R])
            if 0 <= g - LAG_T < n:
                name, p = order[g - LAG_T]
                steps.append(("T", name, p))
                if p % 2:
                    waiting.append(("AV", name, p // 2))
        steps.extend(pending)

    if a:
        attend(order)
        steps += [job("vc"), job("kc"), job("wo"), ("LN", "ln0", 0)]
    else:
        attend(order[:PAIRS])
        attend(order[PAIRS:])
    return steps


class Body:

    def __init__(self, a, b, before=None):
        self.a, self.b, self.before = a, b, before
        self.steps = schedule(a is not None, b is not None)
        self.pairs = [s[1:] for s in self.steps if s[0] == "S"]

    def batch(self, name):
        return self.a if name in STREAM_A else self.b

    def slot(self, name, p, ring):
        return self.pairs.index((name, p)) % ring

    def earlier(self, step, back, same):
        mine = [s for s in self.steps if same(s)]
        i = mine.index(step) - back
        if i >= 0:
            return mine[i], self.batch(mine[i][1])
        if self.before is None:
            return None
        last = [s for s in schedule(True, False) if same(s)][i]
        assert last[1] in STREAM_A and last == [s for s in schedule(True, True) if same(s)][i]
        return last, self.before


def program(nc, io):
    with ExitStack() as ctx:
        def sb(name, shape, dt=F32):
            return ctx.enter_context(nc.sbuf_tensor(name, shape, dt))

        def sem(name):
            return ctx.enter_context(nc.semaphore(name))

        wq0, wk0, wv0 = (sb(n, [P, DT, INNER]) for n in ("wq0", "wk0", "wv0"))
        wo0 = sb("wo0", [P, INNER // P, D])
        w1 = {n: sb("w_" + n, [P, DT, D]) for n in ("q", "k", "v", "cq", "ck", "cv")}
        w1o = {n: sb("w_" + n, [P, QUADS, D]) for n in ("o", "co")}
        wl1 = sb("wl1", [P, DT, FF])
        wl2 = sb("wl2", [P, FF // P, D])
        col = {n: sb("col_" + n, [P, k]) for n, k in
               (("bq0", 8), ("bk0", 8), ("q", DT), ("k", DT), ("cq", DT), ("ck", DT), ("l1", FF // P))}
        row = {n: sb("row_" + n, [P, k]) for n, k in
               (("bv0", INNER), ("bo0", D), ("v", D), ("o", D), ("cv", D), ("co", D), ("l2", D),
                ("g0", D), ("b0", D), ("g1", D), ("b1", D), ("g2", D), ("b2", D), ("g3", D), ("b3", D))}
        ident = sb("ident", [P, P])
        head_rows = sb("head_rows", [P, P // DH1])
        zero = sb("zero", [P, 1])
        minus_half, eps = sb("minus_half", [P, TT]), sb("eps", [P, TT])

        x_tok, c_tok = sb("x_tok", [P, TT, D]), sb("c_tok", [P, TT, D])
        mask_u8 = sb("mask_u8", [P, TT, TOK], U8)
        mask_a = sb("mask_a", [P, TT, TOK], BF16)
        mask_b = sb("mask_b", [P, TT, TOK], BF16)
        x_t, c_t = sb("x_t", [P, DT, TOK]), sb("c_t", [P, DT, TOK])
        qz0 = sb("qz0", [P, HEADS, TOK])
        k0_ctx = sb("k0_ctx", [P, PAIRS, TOK])
        v0 = sb("v0", [P, TT, INNER])
        prob = sb("prob", [P, P_RING, 2, TT, TOK])
        prob_t = sb("prob_t", [P, PT_RING, 2, TT, TOK])
        ext, sums, recip = (sb(n, [P, P_RING, 2, TT]) for n in ("ext", "sums", "recip"))
        q1 = sb("q1", [P, DT, TOK])
        qz1 = sb("qz1", [P, HEADS, TOK])
        h_t = qz1[:, 0:FF // P, :]
        k_t = {"B": sb("k_self", [P, DT, TOK]), "C": sb("k_cross", [P, DT, TOK])}
        v_pad = {"B": sb("v_self", [P, TT, HEADS, SLOT]), "C": sb("v_cross", [P, TT, HEADS, SLOT])}
        ctx1 = sb("ctx1", [P, QUADS, TOK])
        y_a, y_b = sb("y_a", [P, TT, D]), sb("y_b", [P, TT, D])
        res_a, res_ab, res_b = (sb(n, [P, TT, D]) for n in ("res_a", "res_ab", "res_b"))
        y_out = sb("y_out", [P, TT, D])
        xb_t = sb("xb_t", [P, DT, TOK])
        stats = {s: sb("stats_" + s, [P, TT, 6]) for s in "ab"}
        mv = {s: sb("mv_" + s, [P, TT, 2]) for s in "ab"}
        rstd = {s: sb("rstd_" + s, [P, TT]) for s in "ab"}
        var_eps = {s: sb("var_eps_" + s, [P, TT]) for s in "ab"}

        bank = lambda n: ctx.enter_context(nc.psum_tensor(n, [P, 512], F32))
        ps_s = [bank("ps_s0"), bank("ps_s1")]
        ps_t = [bank("ps_t0"), bank("ps_t1")]
        ps_av = bank("ps_av")
        ps_gd = [bank("ps_gd0"), bank("ps_gd1")]
        ps_ga = bank("ps_ga")
        two = lambda t: t[:, :].rearrange("p (a n) -> p a n", a=2)

        w_in = {n: sem("w_in_" + n) for n in ("proj0", "out0", "attn1", "mlp", "small", "mask")}
        x_in, m_in = sem("x_in"), sem("m_in")
        out_done = sem("out_done")
        const_ready = sem("const_ready")
        dve_const = sem("dve_const")
        mask_read = sem("mask_read")
        mask_b_ready = sem("mask_b_ready")
        pool_step = sem("pool_step")
        att = "ABC"
        small = len(col) + len(row)
        scored = {s: sem("scored_" + s) for s in att}
        masked = {s: sem("masked_" + s) for s in att}
        exped = {s: sem("exped_" + s) for s in att}
        recipd = {s: sem("recipd_" + s) for s in att}
        normed = {s: sem("normed_" + s) for s in att}
        turned = {s: sem("turned_" + s) for s in att}
        pt_act = {s: sem("pt_act_" + s) for s in att}
        pt_dve = {s: sem("pt_dve_" + s) for s in att}
        weighed = {s: sem("weighed_" + s) for s in att}
        ctx_out = {s: sem("ctx_out_" + s) for s in att}
        filled = {n: sem("filled_" + n) for n in {**DVE_JOBS, **ACT_JOBS}}
        taken = {n: sem("taken_" + n) for n in {**DVE_JOBS, **ACT_JOBS}}
        q_spread = {s: sem("q_spread_" + s) for s in "BC"}
        lns = ("ln0", "ln1", "ln2", "ln3")
        ln_dve = {n: sem("dve_" + n) for n in lns}
        ln_rstd = {n: sem("rstd_" + n) for n in lns}
        res_ready = {n: sem("res_" + n) for n in ("x", "ln0", "ln1", "ln2")}

        tok_view = lambda t: t.rearrange("b (t p) d -> p b t d", p=P)
        x_d, c_d, m_d, o_d = (tok_view(io[n]) for n in
                              ("x", "ctx_1024", "mask_BxSxS2_bf0", "out"))
        wide = lambda n: io[n].rearrange("(k p) n -> p k n", p=P)
        column = lambda n: io[n].rearrange("(k p) -> p k", p=P)
        L0, L1 = "L0_xattn_", "L1_xattn_"

        def count(b, per, n):
            return b * per + n

        def jobs_of(name):
            return DVE_JOBS.get(name) or ACT_JOBS[name]

        ring = {**{n: (lambda s: s[0] == "J" and s[1] in DVE_JOBS) for n in DVE_JOBS},
                **{n: (lambda s: s[0] == "J" and s[1] in ACT_JOBS) for n in ACT_JOBS}}

        def bank_of(body, step):
            if step[1] in ACT_JOBS:
                return ps_ga
            mine = [s for s in body.steps if ring[step[1]](s)]
            return ps_gd[mine.index(step) % 2]

        LN_AFTER = {"wo": "ln0", "os": "ln1", "oc": "ln2", "y": "ln3"}
        LN_ROWS = {"ln0": ("g0", "b0"), "ln1": ("g1", "b1"), "ln2": ("g2", "b2"), "ln3": ("g3", "b3")}
        NEXT_BIAS = {"ln0": "o", "ln1": "co", "ln2": "l2"}

        def bodies(eng):
            yield Body(0, None)
            with eng.Fori(0, BATCH - 1) as it:
                yield Body(it + 1, it, before=it)
            yield Body(None, BATCH - 1, before=BATCH - 1)

        block = ctx.enter_context(nc.Block())

        @block.sync
        def _(sp):
            def load_x(b):
                sp.dma_start(x_tok[:, :, :], x_d[:, b]).then_inc(x_in, 16)
                sp.dma_start(c_tok[:, :, :], c_d[:, b]).then_inc(x_in, 16)

            def load_mask(b):
                sp.dma_start(mask_u8[:, :, :], m_d[:, b]).then_inc(m_in, 16)

            def load_next(b):
                sp.wait_ge(filled["cT"], count(b, 1, 0))
                sp.wait_ge(res_ready["x"], count(b, 1, 0))
                sp.dma_start(x_tok[:, :, :].unsqueeze(1), x_d[:, bass.ds(b, 1)]).then_inc(x_in, 16)
                sp.dma_start(c_tok[:, :, :].unsqueeze(1), c_d[:, bass.ds(b, 1)]).then_inc(x_in, 16)
                sp.wait_ge(mask_read, count(b, 1, 0))
                sp.dma_start(mask_u8[:, :, :].unsqueeze(1), m_d[:, bass.ds(b, 1)]).then_inc(m_in, 16)

            def store(b):
                sp.wait_ge(ln_dve["ln3"], count(b, 5, 5))
                sp.dma_start(o_d[:, bass.ds(b, 1)], y_out[:, :, :].unsqueeze(1)).then_inc(out_done, 16)

            load_x(0)
            load_mask(0)
            sp.dma_start(q1[:, :, :].bitcast(I32), io["mask_SxS_ik1"].rearrange("(t p) k -> p t k", p=P)
                         ).then_inc(w_in["mask"], 16)
            for w, n in ((wq0, "Wq"), (wk0, "Wk"), (wv0, "Wv")):
                sp.dma_start(w[:, :, :], wide(L0 + n)).then_inc(w_in["proj0"], 16)
            sp.dma_start(wo0[:, :, :], wide(L0 + "Wo")).then_inc(w_in["out0"], 16)
            for n in w1:
                sp.dma_start(w1[n][:, :, :], wide(f"{L1}{n}_w")).then_inc(w_in["attn1"], 16)
            sp.wait_ge(const_ready, 1)
            for n in w1o:
                src = io[f"{L1}{n}_w"].rearrange("(q j d) n -> j d q n", j=4, d=DH1)
                for j in range(4):
                    sp.dma_start(w1o[n][j * SLOT:j * SLOT + DH1, :, :], src[j]).then_inc(w_in["attn1"], 16)
            sp.dma_start(wl1[:, :, :], wide(L1 + "lin1_w")).then_inc(w_in["mlp"], 16)
            sp.dma_start(wl2[:, :, :], wide(L1 + "lin2_w")).then_inc(w_in["mlp"], 16)
            load_next(1)
            with sp.Fori(2, BATCH) as b:
                load_next(b)
                store(b - 2)
            store(BATCH - 2)
            store(BATCH - 1)
            sp.wait_ge(out_done, 16 * BATCH + 16)

        @block.tensor
        def _(pe):
            def wait_bank_free(body, step):
                last = body.earlier(step, 2 if step[1] in DVE_JOBS else 1, ring[step[1]])
                if last:
                    (_, name, i), b = last
                    pe.wait_ge(taken[name], count(b, jobs_of(name), i + 1))

            def product(out, lhs, rhs):
                n = len(lhs)
                for i in range(n):
                    last = nc.tensor.matmul(out, lhs[i], rhs[i], start=i == 0, stop=i == n - 1)
                return last

            def transposes(ps, src):
                for d in range(DT):
                    for t in range(TT):
                        last = nc.tensor.transpose(ps[:, d, t * P:(t + 1) * P],
                                                   src[:, t, d * P:(d + 1) * P], ident[:, :])
                return last

            def columns_out(ps, w, first, src):
                for m in range(2):
                    c = (first + m) * P
                    last = product(ps[:, m, :], [w[:, d, c:c + P] for d in range(DT)],
                                   [src[:, d, :] for d in range(DT)])
                return last

            def tokens_out(ps, src, w):
                n = src.shape[1]
                for t in range(TT):
                    last = product(ps[:, t, :], [src[:, d, t * P:(t + 1) * P] for d in range(n)],
                                   [w[:, d, :] for d in range(n)])
                return last

            def job(body, step):
                _, name, i = step
                b = body.batch(name)
                first = body.before is None
                ps = two(bank_of(body, step))
                wait_bank_free(body, step)
                if name == "xT":
                    pe.wait_ge(x_in, count(b, 32, 32))
                    last = transposes(ps, x_tok)
                elif name == "cT":
                    last = transposes(ps, c_tok)
                elif name in ("q", "k"):
                    pe.wait_ge(taken["xT" if name == "q" else "cT"], count(b, 1, 1))
                    if first:
                        pe.wait_ge(w_in["proj0"], 48)
                    last = columns_out(ps, wq0 if name == "q" else wk0, 2 * i, x_t if name == "q" else c_t)
                elif name == "v":
                    pe.wait_ge(taken["cT"], count(b, 1, 1))
                    t, half = i // 2, i % 2
                    last = product(bank_of(body, step)[:, :], [c_t[:, d, t * P:(t + 1) * P] for d in range(DT)],
                                   [wv0[:, d, half * 512:half * 512 + 512] for d in range(DT)])
                elif name == "kc":
                    if first:
                        pe.wait_ge(w_in["attn1"], 16 * 14)
                    last = columns_out(ps, w1["ck"], 0, c_t)
                elif name == "vc":
                    if first:
                        pe.wait_ge(w_in["attn1"], 16 * 14)
                    last = tokens_out(ps, c_t, w1["cv"])
                elif name == "wo":
                    pe.wait_ge(ctx_out["A"], count(b, QUADS, QUADS))
                    if first:
                        pe.wait_ge(w_in["out0"], 16)
                    last = tokens_out(ps, k0_ctx, wo0)
                elif name == "x1T":
                    pe.wait_ge(ln_dve["ln0"], count(b, 5, 5))
                    last = transposes(ps, y_a)
                elif name in ("x2T", "x3T"):
                    pe.wait_ge(ln_dve["ln1" if name == "x2T" else "ln2"], count(b, 5, 5))
                    last = transposes(ps, y_b)
                elif name in ("qs", "ks", "qc"):
                    pe.wait_ge(taken["x2T" if name == "qc" else "x1T"], count(b, 1, 1))
                    last = columns_out(ps, w1[{"qs": "q", "ks": "k", "qc": "cq"}[name]], 0, xb_t)
                elif name == "vs":
                    last = tokens_out(ps, xb_t, w1["v"])
                elif name in ("os", "oc"):
                    s = "B" if name == "os" else "C"
                    pe.wait_ge(ctx_out[s], count(b, QUADS, QUADS))
                    last = tokens_out(ps, ctx1, w1o["o" if name == "os" else "co"])
                elif name == "h":
                    pe.wait_ge(taken["x3T"], count(b, 1, 1))
                    if i == 0:
                        pe.wait_ge(w_in["mlp"], 32)
                    last = columns_out(ps, wl1, 2 * i, xb_t)
                elif name == "y":
                    pe.wait_ge(taken["h"], count(b, 4, 4))
                    last = tokens_out(ps, h_t, wl2)
                last.then_inc(filled[name], 1)

            def scores(body, step):
                _, s, p = step
                b = body.batch(s)
                if s == "A":
                    pe.wait_ge(taken["q"], count(b, 4, p // 2 + 1))
                    pe.wait_ge(taken["k"], count(b, 4, p // 2 + 1))
                else:
                    pe.wait_ge(q_spread[s], count(b, 2, p // 4 + 1))
                    if s == "B":
                        pe.wait_ge(taken["ks"], count(b, 1, 1))
                    else:
                        pe.wait_ge(taken["kc"], count(b, 1, 1))
                last_pair = body.earlier(step, 1, lambda x: x[0] == "S")
                for e in range(2):
                    if last_pair:
                        (_, s0, p0), b0 = last_pair
                        pe.wait_ge(masked[s0], count(b0, HEADS, 2 * p0 + e + 1))
                    h = 2 * p + e
                    q, k = (qz0, k0_ctx[:, p, :]) if s == "A" else (qz1, k_t[s][:, h // 8, :])
                    for t in range(TT):
                        last = nc.tensor.matmul(two(ps_s[e])[:, t, :], q[:, h, t * P:(t + 1) * P], k,
                                                start=True, stop=True)
                    last.then_inc(scored[s], 1)

            def turn(body, step):
                _, s, p = step
                b = body.batch(s)
                src = prob[:, body.slot(s, p, P_RING)]
                pe.wait_ge(normed[s], count(b, PAIRS, p + 1))
                last_pair = body.earlier(step, 1, lambda x: x[0] == "T")
                for e in range(2):
                    if last_pair:
                        (_, s0, p0), b0 = last_pair
                        pe.wait_ge((pt_act, pt_dve)[e][s0], count(b0, PAIRS, p0 + 1))
                    for kt in range(TT):
                        for qt in range(TT):
                            last = nc.tensor.transpose(two(ps_t[e])[:, kt, qt * P:(qt + 1) * P],
                                                       src[:, e, qt, kt * P:(kt + 1) * P], ident[:, :])
                    last.then_inc(turned[s], 1)

            def weigh(body, step):
                _, s, quad = step
                b = body.batch(s)
                pe.wait_ge(pt_act[s], count(b, PAIRS, 2 * quad + 2))
                pe.wait_ge(pt_dve[s], count(b, PAIRS, 2 * quad + 2))
                if s == "A":
                    pe.wait_ge(taken["v"], count(b, 4, 4))
                else:
                    pe.wait_ge(taken["vs" if s == "B" else "vc"], count(b, 1, 1))
                last_quad = body.earlier(step, 1, lambda x: x[0] == "AV")
                if last_quad:
                    (_, s0, q0), b0 = last_quad
                    pe.wait_ge(ctx_out[s0], count(b0, QUADS, q0 + 1))
                if s == "A":
                    for j in range(2):
                        pt = prob_t[:, body.slot(s, 2 * quad + j, PT_RING)]
                        for kt in range(TT):
                            for e in range(2):
                                h = 4 * quad + 2 * j + e
                                last = nc.tensor.matmul(two(ps_av)[e * DH0:(e + 1) * DH0, j, :],
                                                        v0[:, kt, h * DH0:(h + 1) * DH0], pt[:, e, kt, :],
                                                        start=kt == 0, stop=kt == TT - 1)
                else:
                    for kt in range(TT):
                        for j in range(4):
                            pt = prob_t[:, body.slot(s, 2 * quad + j // 2, PT_RING)]
                            last = nc.tensor.matmul(ps_av[j * SLOT:(j + 1) * SLOT, 0:TOK],
                                                    v_pad[s][:, kt, 4 * quad + j, :], pt[:, j % 2, kt, :],
                                                    start=kt == 0, stop=kt == TT - 1,
                                                    tile_position=(0, j * SLOT))
                last.then_inc(weighed[s], 1)

            pe.wait_ge(const_ready, 2)
            for body in bodies(pe):
                for step in body.steps:
                    {"J": job, "S": scores, "T": turn, "AV": weigh}.get(step[0], lambda *_: None)(body, step)

        @block.scalar
        def _(act):
            act.dma_start(col["bq0"][:, :], column(L0 + "bq"), allow_slow_non_contiguous=True).then_inc(w_in["small"], 16)
            act.dma_start(col["bk0"][:, :], column(L0 + "bk"), allow_slow_non_contiguous=True).then_inc(w_in["small"], 16)
            for n in ("q", "k", "cq", "ck"):
                act.dma_start(col[n][:, :], column(f"{L1}{n}_b"), allow_slow_non_contiguous=True).then_inc(w_in["small"], 16)
            act.dma_start(col["l1"][:, :], column(L1 + "lin1_b"), allow_slow_non_contiguous=True).then_inc(w_in["small"], 16)
            for n, src in (("bv0", L0 + "bv"), ("bo0", L0 + "bo"), ("v", L1 + "v_b"), ("o", L1 + "o_b"),
                           ("cv", L1 + "cv_b"), ("co", L1 + "co_b"), ("l2", L1 + "lin2_b"),
                           ("g0", L0 + "gamma"), ("b0", L0 + "beta"), ("g1", L1 + "ln1_g"),
                           ("b1", L1 + "ln1_b"), ("g2", L1 + "ln2_g"), ("b2", L1 + "ln2_b"),
                           ("g3", L1 + "ln3_g"), ("b3", L1 + "ln3_b")):
                act.dma_start(row[n][:, :], io[src].partition_broadcast(P)).then_inc(w_in["small"], 16)
            act.wait_ge(w_in["small"], 16 * small)

            def job(body, step):
                _, name, i = step
                b = body.batch(name)
                if name not in ACT_JOBS:
                    return
                ps = two(ps_ga)
                act.wait_ge(filled[name], count(b, jobs_of(name), i + 1))
                if name in ("xT", "cT", "x1T", "x2T", "x3T"):
                    out = {"xT": x_t, "cT": c_t}.get(name, xb_t)
                    nc.scalar.activation(out[:, :, :], ps, ACT.Copy).then_inc(taken[name], 1)
                    return
                out, bias = {"k": (k0_ctx, col["bk0"]), "kc": (k_t["C"], col["ck"]),
                             "ks": (k_t["B"], col["k"]), "h": (h_t, col["l1"])}[name]
                for m in range(2):
                    c = 2 * i + m
                    last = nc.scalar.activation(out[:, c, :], ps[:, m, :],
                                                ACT.Relu if name == "h" else ACT.Identity,
                                                bias=bias[:, c:c + 1])
                last.then_inc(taken[name], 1)

            def exps(body, step):
                _, s, p = step
                b = body.batch(s)
                slot = body.slot(s, p, P_RING)
                for e in range(2):
                    act.wait_ge(masked[s], count(b, HEADS, 2 * p + e + 1))
                    for t in range(TT):
                        tile = prob[:, slot, e, t, :]
                        last = nc.scalar.activation(tile, tile, ACT.Exp, bias=ext[:, slot, e, t:t + 1],
                                                    scale=-1.0, accum_out=sums[:, slot, e, t:t + 1])
                last.then_inc(exped[s], 1)

            def evac_turned(body, step):
                _, s, p = step
                act.wait_ge(turned[s], count(body.batch(s), HEADS, 2 * p + 1))
                nc.scalar.activation(prob_t[:, body.slot(s, p, PT_RING), 0], two(ps_t[0]),
                                     ACT.Copy).then_inc(pt_act[s], 1)

            def evac_weighed(body, step):
                _, s, quad = step
                act.wait_ge(weighed[s], count(body.batch(s), QUADS, quad + 1))
                if s == "A":
                    out, src = k0_ctx[:, 2 * quad:2 * quad + 2, :], two(ps_av)
                else:
                    out, src = ctx1[:, quad, :], ps_av[:, 0:TOK]
                nc.scalar.activation(out, src, ACT.Copy).then_inc(ctx_out[s], 1)

            for body in bodies(act):
                for step in body.steps:
                    {"J": job, "S": exps, "T": evac_turned, "AV": evac_weighed}.get(
                        step[0], lambda *_: None)(body, step)

        @block.vector
        def _(dve):
            dve.wait_ge(w_in["small"], 16 * small)
            for n in "BC":
                nc.vector.memset(v_pad[n][:, :, :, DH1:SLOT], 0.0)
            nc.vector.memset(qz0[DH0:P, 0:HEADS:2, :], 0.0)
            nc.vector.memset(qz0[0:DH0, 1:HEADS:2, :], 0.0)
            nc.vector.memset(eps[:, :], EPS)
            nc.vector.memset(minus_half[:, :], -0.5)
            nc.vector.memset(zero[:, :], 0.0).then_inc(out_done, 16)
            dve.wait_ge(out_done, 16)
            nc.vector.memset(mv["a"][:, :, :], 0.0).then_inc(dve_const, 1)
            dve.wait_ge(const_ready, 3)
            dve.wait_ge(w_in["mask"], 16)
            nc.vector.tensor_scalar(mask_b[:, :, :], q1[:, :, :].bitcast(I32), 0.0, -BIG,
                                    ALU.not_equal, ALU.mult).then_inc(mask_b_ready, 1)
            dve.wait_ge(mask_b_ready, 1)

            def held(value):
                return value if isinstance(value, int) else dve.to_reg(value)

            def job(body, step):
                _, name, i = step
                b = body.batch(name)
                if name == "cT":
                    dve.wait_ge(m_in, count(b, 16, 16))
                    nc.vector.tensor_scalar(mask_a[:, :, :], mask_u8[:, :, :], 0.0, -BIG,
                                            ALU.not_equal, ALU.mult).then_inc(mask_read, 1)
                if name not in DVE_JOBS:
                    return
                bank = bank_of(body, step)
                ps = two(bank)
                dve.wait_ge(filled[name], count(b, jobs_of(name), i + 1))
                if name == "q":
                    for e in range(2):
                        r = slice(e * DH0, (e + 1) * DH0)
                        bias = col["bq0"][r, 2 * i:2 * i + 2].unsqueeze(2).to_broadcast([DH0, 2, TOK])
                        last = nc.vector.tensor_tensor(qz0[r, 4 * i + e:4 * i + 4:2, :], ps[r], bias, ALU.add)
                    last.then_inc(taken[name], 1)
                elif name == "v":
                    t, half = i // 2, i % 2
                    cols = slice(half * 512, half * 512 + 512)
                    nc.vector.tensor_tensor(v0[:, t, cols], bank[:, :], row["bv0"][:, cols],
                                            ALU.add).then_inc(taken[name], 1)
                elif name in ("vs", "vc"):
                    s, bias = ("B", row["v"]) if name == "vs" else ("C", row["cv"])
                    for t in range(TT):
                        last = nc.vector.tensor_tensor(
                            v_pad[s][:, t, :, 0:DH1], ps[:, t, :].rearrange("p (h d) -> p h d", h=HEADS),
                            bias[:, :].rearrange("p (h d) -> p h d", h=HEADS), ALU.add)
                    last.then_inc(taken[name], 1)
                elif name in ("qs", "qc"):
                    s, bias = ("B", col["q"]) if name == "qs" else ("C", col["cq"])
                    nc.vector.tensor_tensor(q1[:, :, :], ps, bias[:, :].unsqueeze(2).to_broadcast([P, DT, TOK]),
                                            ALU.add).then_inc(taken[name], 1)
                    dve.wait_ge(taken[name], count(b, 1, 1))
                    for d in range(DT):
                        nc.vector.tensor_tensor(
                            qz1[:, 8 * d:8 * d + 8, :], q1[:, d, :].unsqueeze(1).to_broadcast([P, 8, TOK]),
                            head_rows[:, :].unsqueeze(2).to_broadcast([P, 8, TOK]),
                            ALU.mult).then_inc(q_spread[s], 1)
                else:
                    residual(name, b, ps)

            def residual(name, b, ps):
                ln = LN_AFTER[name]
                k, y, res = ("a", y_a, res_a) if ln == "ln0" else ("b", y_b, {"ln1": res_ab}.get(ln, res_b))
                before = {"ln0": "x", "ln1": "ln0", "ln2": "ln1", "ln3": "ln2"}[ln]
                dve.wait_ge(res_ready[before], count(b, 1, 1))
                nc.vector.tensor_tensor(y[:, :, :], ps, res[:, :, :], ALU.add).then_inc(taken[name], 1)
                dve.wait_ge(taken[name], count(b, 1, 1))
                for t in range(TT):
                    last = nc.vector.bn_stats(stats[k][:, t, :], y[:, t, :])
                last.then_inc(ln_dve[ln], 1)
                value = held(count(b, 5, 1))
                dve.wait_ge(const_ready, 3)
                dve.wait_ge(ln_dve[ln], value)
                for t in range(TT):
                    last = nc.vector.bn_aggr(mv[k][:, t, :], stats[k][:, t, :])
                last.then_inc(ln_dve[ln], 1)

            def layer_norm(body, step):
                ln = step[1]
                b = body.a if ln == "ln0" else body.b
                k, y = ("a", y_a) if ln == "ln0" else ("b", y_b)
                g, beta = (row[n][:, :].unsqueeze(1).to_broadcast([P, TT, D]) for n in LN_ROWS[ln])
                dve.wait_ge(ln_rstd[ln], count(b, 2, 2))
                for t in range(TT):
                    last = nc.vector.tensor_scalar(y[:, t, :], y[:, t, :], mv[k][:, t, 0:1],
                                                   rstd[k][:, t:t + 1], ALU.subtract, ALU.mult)
                last.then_inc(ln_dve[ln], 1)
                dve.wait_ge(ln_dve[ln], count(b, 5, 3))
                nc.vector.tensor_tensor(y[:, :, :], y[:, :, :], g, ALU.mult).then_inc(ln_dve[ln], 1)
                dve.wait_ge(ln_dve[ln], count(b, 5, 4))
                out = y
                if ln == "ln3":
                    dve.wait_ge(out_done, count(b, 16, 16))
                    out = y_out
                nc.vector.tensor_tensor(out[:, :, :], y[:, :, :], beta, ALU.add).then_inc(ln_dve[ln], 1)

            def extremes(body, step):
                _, s, p = step
                b = body.batch(s)
                slot = body.slot(s, p, P_RING)
                if s == "A" and p == 0:
                    dve.wait_ge(mask_read, count(b, 1, 1))
                for e in range(2):
                    value = held(count(b, HEADS, 2 * p + e + 1))
                    dve.wait_ge(const_ready, 3)
                    dve.wait_ge(scored[s], value)
                    for t in range(TT):
                        mask = {"A": mask_a[:, t, :], "B": mask_b[:, t, :],
                                "C": zero[:, :].to_broadcast([P, TOK])}[s]
                        last = nc.vector.tensor_tensor_reduce(
                            out=prob[:, slot, e, t, :], in0=two(ps_s[e])[:, t, :], in1=mask,
                            scale=-SCALE[s], scalar=BIG, op0=ALU.add, op1=ALU.min,
                            accum_out=ext[:, slot, e, t:t + 1])
                    last.then_inc(masked[s], 1)

            def reciprocals(body, step):
                _, s, p = step
                slot = body.slot(s, p, P_RING)
                dve.wait_ge(exped[s], count(body.batch(s), PAIRS, p + 1))
                nc.vector.reciprocal(recip[:, slot], sums[:, slot]).then_inc(recipd[s], 1)

            def evac_turned(body, step):
                _, s, p = step
                dve.wait_ge(turned[s], count(body.batch(s), HEADS, 2 * p + 2))
                nc.vector.tensor_copy(prob_t[:, body.slot(s, p, PT_RING), 1], two(ps_t[1])).then_inc(pt_dve[s], 1)

            for body in bodies(dve):
                for step in body.steps:
                    {"J": job, "LN": layer_norm, "S": extremes, "R": reciprocals, "T": evac_turned}.get(
                        step[0], lambda *_: None)(body, step)

        @block.gpsimd
        def _(pool):
            nc.gpsimd.memset(w1o["o"][:, :, :], 0.0).then_inc(pool_step, 1)
            pool.wait_ge(pool_step, 1)
            nc.gpsimd.memset(w1o["co"][:, :, :], 0.0).then_inc(const_ready, 1)
            pool.wait_ge(const_ready, 1)
            nc.gpsimd.memset(ident[:, :], 1.0).then_inc(pool_step, 1)
            pool.wait_ge(pool_step, 2)
            nc.gpsimd.affine_select(out=ident[:, :], in_=ident[:, :], compare_op=ALU.is_equal, fill=0.0,
                                    base=0, pattern=[[-1, P]], channel_multiplier=1).then_inc(const_ready, 1)
            pool.wait_ge(const_ready, 2)
            nc.gpsimd.memset(head_rows[:, :], 1.0).then_inc(pool_step, 1)
            pool.wait_ge(pool_step, 3)
            nc.gpsimd.affine_select(out=head_rows[:, :], in_=head_rows[:, :], compare_op=ALU.is_ge, fill=0.0,
                                    base=0, pattern=[[-DH1, P // DH1]], channel_multiplier=1).then_inc(pool_step, 1)
            pool.wait_ge(pool_step, 4)
            nc.gpsimd.affine_select(out=head_rows[:, :], in_=head_rows[:, :], compare_op=ALU.is_ge, fill=0.0,
                                    base=DH1 - 1, pattern=[[DH1, P // DH1]],
                                    channel_multiplier=-1).then_inc(const_ready, 1)
            pool.wait_ge(w_in["small"], 16 * small)
            pool.wait_ge(dve_const, 1)

            def job(body, step):
                _, name, i = step
                b = body.batch(name)
                if name == "xT":
                    pool.wait_ge(x_in, count(b, 32, 32))
                    nc.gpsimd.tensor_tensor(res_a[:, :, :], x_tok[:, :, :],
                                            row["bo0"][:, :].unsqueeze(1).to_broadcast([P, TT, D]),
                                            ALU.add).then_inc(res_ready["x"], 1)
                elif name in LN_AFTER:
                    ln = LN_AFTER[name]
                    k = "a" if ln == "ln0" else "b"
                    pool.wait_ge(ln_dve[ln], count(b, 5, 2))
                    nc.gpsimd.tensor_tensor(var_eps[k][:, :], mv[k][:, :, 1], eps[:, :],
                                            ALU.add).then_inc(ln_rstd[ln], 1)
                    pool.wait_ge(ln_rstd[ln], count(b, 2, 1))
                    nc.gpsimd.tensor_tensor(rstd[k][:, :], var_eps[k][:, :], minus_half[:, :],
                                            ALU.pow).then_inc(ln_rstd[ln], 1)

            def next_residual(body, step):
                ln = step[1]
                if ln not in NEXT_BIAS:
                    return
                b = body.a if ln == "ln0" else body.b
                y, out = (y_a, res_ab) if ln == "ln0" else (y_b, res_b)
                pool.wait_ge(ln_dve[ln], count(b, 5, 5))
                nc.gpsimd.tensor_tensor(out[:, :, :], y[:, :, :],
                                        row[NEXT_BIAS[ln]][:, :].unsqueeze(1).to_broadcast([P, TT, D]),
                                        ALU.add).then_inc(res_ready[ln], 1)

            def normalize(body, step):
                _, s, p = step
                slot = body.slot(s, p, P_RING)
                pool.wait_ge(recipd[s], count(body.batch(s), PAIRS, p + 1))
                flat = prob[:, slot].rearrange("p e t k -> p (e t) k")
                nc.gpsimd.tensor_tensor(flat, flat,
                                        recip[:, slot].rearrange("p e t -> p (e t)").unsqueeze(2)
                                        .to_broadcast([P, 2 * TT, TOK]), ALU.mult).then_inc(normed[s], 1)

            for body in bodies(pool):
                for step in body.steps:
                    {"J": job, "LN": next_residual, "R": normalize}.get(
                        step[0], lambda *_: None)(body, step)


_OUT = (BATCH, TOK, D)


def kernel(**inputs):
    import concourse.bacc as bacc
    from concourse.bass_utils import run_bass_kernel_spmd

    nc = bacc.Bacc("TRN2", target_bir_lowering=False, num_devices=1)
    arrays = {n: np.ascontiguousarray(a) for n, a in inputs.items()}
    io = {n: nc.dram_tensor(n, a.shape, mybir.dt.from_np(a.dtype), kind="ExternalInput").ap()
          for n, a in arrays.items()}
    io["out"] = nc.dram_tensor("out", _OUT, F32, kind="ExternalOutput").ap()
    program(nc, io)
    return run_bass_kernel_spmd(nc, [arrays], core_ids=[0]).results[0]["out"]
```

```python
from contextlib import ExitStack

import numpy as np

import concourse.bass as bass
from concourse import mybir

ALU = mybir.AluOpType
ACT = mybir.ActivationFunctionType
F32 = mybir.dt.float32
F32R = mybir.dt.float32r
BF16 = mybir.dt.bfloat16
I32 = mybir.dt.int32
U8 = mybir.dt.uint8

P = 128
BATCH, TOK, D = 16, 256, 256
TT, DT = TOK // P, D // P
HEADS = 16
PAIRS, QUADS = HEADS // 2, HEADS // 4
DH0, DH1 = 64, D // HEADS
INNER = HEADS * DH0
FF = 1024
SLOT = 32
EPS = 1e-5
BIG = 2.0 ** 127
SCALE = {"A": DH0 ** -0.5, "B": DH1 ** -0.5, "C": DH1 ** -0.5}

P_RING, PT_RING = 4, 3
LAG_R = 1

DVE_JOBS = {"q": 4, "v": 4, "kc": 1, "wo": 1, "qs": 1, "ks": 1, "os": 1, "qc": 1, "oc": 1, "hd": 2,
            "y": 1}
ACT_JOBS = {"xT": 1, "cT": 1, "k": 4, "vc": 1, "x1T": 1, "vs": 1, "x2T": 1, "x3T": 1, "h": 2}
STREAM_A = {"A", "q", "v", "vc", "wo", "xT", "cT", "k", "kc", "ln0", "load"}
LN_STEPS = {"ln0": 3, "ln1": 3, "ln2": 3, "ln3": 5}
Q0_RING = 2


def schedule(a, b):
    job = lambda name, i=0: ("J", name, i)
    pairs = lambda name, *ps: [(name, p) for p in ps]
    steps = []

    def attend(order, after, late=None, drained=((), (), ())):
        n, late = len(order), late or {}
        turn_at = [g + (3 if all(o[0] != "A" for o in order[g:g + 4]) and g + 4 <= n else 2)
                   for g in range(n)]
        waiting = []
        for g in range(n + 3):
            if g < n:
                steps.append(("S",) + order[g])
            if 0 <= g - LAG_R < n:
                steps.append(("R",) + order[g - LAG_R])
            large = g < n and order[g][0] == "A"
            if large:
                steps.extend(waiting)
                waiting = []
            steps.extend(after.get(order[g], []) if g < n else drained[g - n])
            if g >= n:
                steps.extend(waiting)
                waiting = []
            turned = []
            for i in range(n):
                if turn_at[i] == g:
                    name, p = order[i]
                    steps.append(("T", name, p))
                    steps.extend(waiting)
                    waiting = []
                    if p % 2:
                        turned.append(("AV", name, p // 2))
            waiting += turned
            steps.extend(late.get(order[g], []) if g < n else [])

    k_spread, q_spread = ("DMA", "C", "k"), ("DMA", "C", "q")
    kc = [job("kc"), ("DMA", "C", "save")]
    ends_b = [job("os"), ("LN", "ln1", 0), job("x2T"), job("qc"), q_spread]
    mlp = [job("x3T"), job("h", 0), job("hd", 0), job("h", 1), job("hd", 1)]
    ends_mlp = [job("y"), ("LN", "ln3", 0), ("IO", "store", 0)]
    b_spread = [("DMA", "B", "save"), job("qs"), ("DMA", "B", "q"), job("vs")]
    starts_b = [job("x1T"), job("ks")] + b_spread
    if a and b:
        steps += [job("xT"), job("cT"), ("IO", "load", 0), job("q", 0), job("k", 0), job("v", 0),
                  job("x1T"), job("v", 1), job("ks")] + b_spread + [job("k", 1)]
        attend(pairs("A", 0, 1) + pairs("B", *range(8)) + pairs("A", 2, 3, 4, 5),
               {("A", 1): [job("q", 1)], ("B", 2): [job("q", 2)], ("B", 5): [job("k", 2)],
                ("A", 2): [k_spread], ("A", 5): [("LN", "ln1", 0)]},
               {("A", 4): [job("os")]},
               ([job("x2T"), job("v", 2)], [job("qc"), q_spread, job("v", 3)],
                [job("q", 3), job("k", 3)]))
        attend(pairs("C", *range(8)) + pairs("A", 6, 7), {}, {},
               ([], [job("oc")], [("LN", "ln2", 0)]))
        steps += mlp
        steps += [job("vc"), ends_mlp[0]] + kc + ends_mlp[1:] + [job("wo"), ("LN", "ln0", 0)]
    elif a:
        steps += [job("xT"), job("cT"), ("IO", "load", 0), job("q", 0), job("k", 0), job("q", 1),
                  job("k", 1)] + [job("v", i) for i in range(4)] + [job("k", 2), job("k", 3)]
        attend(pairs("A", *range(8)), {("A", 1): [job("q", 2)], ("A", 3): [job("q", 3)]})
        steps += [job("vc")] + kc + [job("wo"), ("LN", "ln0", 0)]
    else:
        steps += starts_b
        attend(pairs("B", *range(8)), {("B", 7): [k_spread]})
        steps += ends_b
        attend(pairs("C", *range(8)), {})
        steps += [job("oc"), ("LN", "ln2", 0)] + mlp + ends_mlp
    return steps


class Body:

    def __init__(self, a, b, before=None):
        self.a, self.b, self.before = a, b, before
        self.steps = schedule(a is not None, b is not None)
        self.pairs = [s[1:] for s in self.steps if s[0] == "S"]

    def batch(self, name):
        return self.a if name in STREAM_A else self.b

    def slot(self, name, p, ring):
        return self.pairs.index((name, p)) % ring

    def earlier(self, step, back, same):
        mine = [s for s in self.steps if same(s)]
        i = mine.index(step) - back
        if i >= 0:
            return mine[i], self.batch(mine[i][1])
        if self.before is None:
            return None
        last = [s for s in schedule(True, False) if same(s)][i]
        assert last[1] in STREAM_A and last == [s for s in schedule(True, True) if same(s)][i]
        return last, self.before


def program(nc, io):
    with ExitStack() as ctx:
        def sb(name, shape, dt=F32):
            return ctx.enter_context(nc.sbuf_tensor(name, shape, dt))

        def sem(name):
            return ctx.enter_context(nc.semaphore(name))

        wq0, wk0, wv0 = (sb(n, [P, DT, INNER]) for n in ("wq0", "wk0", "wv0"))
        wo0 = sb("wo0", [P, INNER // P, D])
        w1 = {n: sb("w_" + n, [P, DT, D]) for n in ("q", "k", "v", "cq", "ck", "cv")}
        w1o = {n: sb("w_" + n, [P, DT, D]) for n in ("o", "co")}
        wl1 = sb("wl1", [P, DT, FF])
        wl2 = sb("wl2", [P, FF // P, D])
        col = {n: sb("col_" + n, [P, k]) for n, k in
               (("bq0", 8), ("bk0", 8), ("bv0", 8), ("q", DT), ("k", DT), ("cq", DT), ("ck", DT),
                ("l1", FF // P), ("v", DT), ("cv", DT), ("g0", DT), ("b0", DT), ("g1", DT), ("b1", DT), ("g2", DT), ("b2", DT))}
        row = {n: sb("row_" + n, [P, k]) for n, k in
               (("bo0", D), ("g0", D), ("b0", D), ("g1", D), ("b1", D), ("g2", D), ("b2", D), ("g3", D), ("b3", D))}
        ident = sb("ident", [P, P])
        zero = sb("zero", [P, 1])
        minus_half, eps = sb("minus_half", [P, TT]), sb("eps", [P, TT])

        x_tok, c_tok = sb("x_tok", [P, TT, D]), sb("c_tok", [P, TT, D])
        mask_u8 = sb("mask_u8", [P, TT, TOK], U8)
        mask_a = sb("mask_a", [P, TT, TOK], BF16)
        mask_b = sb("mask_b", [P, TT, TOK], BF16)
        x_t, c_t = sb("x_t", [P, DT, TOK]), sb("c_t", [P, DT, TOK])
        qz0 = sb("qz0", [P, Q0_RING * HEADS // 4, TOK])
        k0_ctx = sb("k0_ctx", [P, PAIRS, TOK])
        v0 = sb("v0", [P, TT, INNER])
        prob = sb("prob", [P, P_RING, 2, TT, TOK])
        prob_t = sb("prob_t", [P, PT_RING, 2, TT, TOK])
        ext, sums, recip = (sb(n, [P, P_RING, 2, TT]) for n in ("ext", "sums", "recip"))
        qk = sb("qk", [P, DT, TOK])
        k_hl, q_hl = sb("k_hl", [P, 2, DT, TOK]), sb("q_hl", [P, 2, DT, TOK])
        k4 = sb("k4", [P, PAIRS, TOK], F32R)
        q4 = sb("q4", [P, HEADS, TOK], F32R)
        h_t = sb("h_t", [P, FF // P, TOK])
        v1 = {"B": sb("v_self", [P, TT, HEADS, SLOT]), "C": sb("v_cross", [P, TT, HEADS, SLOT])}
        ctx1 = sb("ctx1", [P, DT, TOK])
        y_a, y_b = sb("y_a", [P, TT, D]), sb("y_b", [P, TT, D])
        res_a, res_ab, res_b = (sb(n, [P, TT, D]) for n in ("res_a", "res_ab", "res_b"))
        y_out = sb("y_out", [P, TT, D])
        xb_t = sb("xb_t", [P, DT, TOK])
        stats = {s: sb("stats_" + s, [P, TT, 6]) for s in "ab"}
        mv = {s: sb("mv_" + s, [P, TT, 2]) for s in "ab"}
        rstd = {s: sb("rstd_" + s, [P, TT]) for s in "ab"}
        var_eps = {s: sb("var_eps_" + s, [P, TT]) for s in "ab"}

        landing = {n: prob[:, 0, 0, 0, :] if i == 0 else prob[:, 0, 0, 1, :] if i == 1 else prob[:, 0, 1, 0, :]
                   for i, n in enumerate(("o", "co", "l2"))}

        bank = lambda n: ctx.enter_context(nc.psum_tensor(n, [P, 512], F32))
        ps_s = [bank("ps_s0"), bank("ps_s1")]
        ps_t = [bank("ps_t0"), bank("ps_t1")]
        ps_av = bank("ps_av")
        ps_gd = [bank("ps_gd0"), bank("ps_gd1")]
        ps_ga = bank("ps_ga")
        two = lambda t: t[:, :].rearrange("p (a n) -> p a n", a=2)

        w_in = {n: sem("w_in_" + n) for n in ("proj0", "out0", "attn1", "rows1", "mlp", "small", "mask")}
        x_in, m_in = sem("x_in"), sem("m_in")
        out_done = sem("out_done")
        const_ready = sem("const_ready")
        dve_const = sem("dve_const")
        mask_read = sem("mask_read")
        mask_b_ready = sem("mask_b_ready")
        pool_step = sem("pool_step")
        att = "ABC"
        small = len(col) - 2 + len(row) + 3
        SPREAD = {"k": 4, "q": 9}
        scored = {s: sem("scored_" + s) for s in att}
        masked = {s: sem("masked_" + s) for s in att}
        exped = {s: sem("exped_" + s) for s in att}
        recipd = {s: sem("recipd_" + s) for s in att}
        normed = {s: sem("normed_" + s) for s in att}
        turned = {s: sem("turned_" + s) for s in att}
        pt_act = {s: sem("pt_act_" + s) for s in att}
        pt_dve = {s: sem("pt_dve_" + s) for s in att}
        weighed = {s: sem("weighed_" + s) for s in att}
        ctx_out = {s: sem("ctx_out_" + s) for s in att}
        CTX_OUTS = {"A": QUADS, "B": DT, "C": DT}
        filled = {n: sem("filled_" + n) for n in {**DVE_JOBS, **ACT_JOBS}}
        taken = {n: sem("taken_" + n) for n in {**DVE_JOBS, **ACT_JOBS}}
        q_split = {s: sem("q_split_" + s) for s in "BC"}
        k_split = {s: sem("k_split_" + s) for s in "BC"}
        k_saved = {s: sem("k_saved_" + s) for s in "BC"}
        spread_k = {s: sem("spread_k_" + s) for s in "BC"}
        spread_q = {s: sem("spread_q_" + s) for s in "BC"}
        k_parts = {s: nc.dram_tensor("k_parts_" + s, (2, D, TOK), F32) for s in "BC"}
        q_parts = nc.dram_tensor("q_parts", (2, D, TOK), F32)
        lns = ("ln0", "ln1", "ln2", "ln3")
        ln_dve = {n: sem("dve_" + n) for n in lns}
        ln_rstd = {n: sem("rstd_" + n) for n in lns}
        res_ready = {n: sem("res_" + n) for n in ("x", "ln0", "ln1", "ln2")}

        tok_view = lambda t: t.rearrange("b (t p) d -> p b t d", p=P)
        x_d, c_d, m_d, o_d = (tok_view(io[n]) for n in
                              ("x", "ctx_1024", "mask_BxSxS2_bf0", "out"))
        wide = lambda n: io[n].rearrange("(k p) n -> p k n", p=P)
        column = lambda n: io[n].rearrange("(k p) -> p k", p=P)
        L0, L1 = "L0_xattn_", "L1_xattn_"

        def count(b, per, n):
            return b * per + n

        def jobs_of(name):
            return DVE_JOBS.get(name) or ACT_JOBS[name]

        ring = {**{n: (lambda s: s[0] == "J" and s[1] in DVE_JOBS) for n in DVE_JOBS},
                **{n: (lambda s: s[0] == "J" and s[1] in ACT_JOBS) for n in ACT_JOBS}}

        def bank_of(body, step):
            if step[1] in ACT_JOBS:
                return ps_ga
            mine = [s for s in body.steps if ring[step[1]](s)]
            return ps_gd[mine.index(step) % 2]

        LN_AFTER = {"wo": "ln0", "os": "ln1", "oc": "ln2", "y": "ln3"}
        LN_ROWS = {"ln0": ("g0", "b0"), "ln1": ("g1", "b1"), "ln2": ("g2", "b2"), "ln3": ("g3", "b3")}

        def bodies(eng, peel_last=False):
            yield Body(0, None)
            with eng.Fori(0, BATCH - 1 - peel_last) as it:
                yield Body(it + 1, it, before=it)
            if peel_last:
                yield Body(BATCH - 1, BATCH - 2, before=BATCH - 2)
            yield Body(None, BATCH - 1, before=BATCH - 1)

        block = ctx.enter_context(nc.Block())

        @block.sync
        def _(sp):
            def load(body, step):
                b = body.a
                if isinstance(b, int) and b == BATCH - 1:
                    return
                sp.wait_ge(filled["cT"], count(b, 1, 1))
                sp.wait_ge(res_ready["x"], count(b, 1, 1))
                sp.dma_start(x_tok[:, :, :].unsqueeze(1), x_d[:, bass.ds(b + 1, 1)]).then_inc(x_in, 16)
                sp.dma_start(c_tok[:, :, :].unsqueeze(1), c_d[:, bass.ds(b + 1, 1)]).then_inc(x_in, 16)
                sp.wait_ge(mask_read, count(b, 1, 1))
                sp.dma_start(mask_u8[:, :, :].unsqueeze(1), m_d[:, bass.ds(b + 1, 1)]).then_inc(m_in, 16)

            def store(body, step):
                b = body.b
                sp.wait_ge(ln_dve["ln3"], count(b, 5, 5))
                sp.dma_start(o_d[:, bass.ds(b, 1)], y_out[:, :, :].unsqueeze(1)).then_inc(out_done, 16)

            def save_keys(body, step):
                s = step[1]
                b = body.b if s == "B" else body.a
                sp.wait_ge(k_split[s], count(b, 2, 2))
                if body.b is not None:
                    if s == "C":
                        sp.wait_ge(spread_k["C"], count(body.b, 16 * SPREAD["k"], 16 * SPREAD["k"]))
                sp.dma_start(k_parts[s][:, :, :].rearrange("a (d p) t -> p (a d) t", p=P),
                             k_hl[:, :, :, :].rearrange("p a d t -> p (a d) t")).then_inc(k_saved[s], 16)

            def spread_keys(body, step):
                s, b = step[1], body.b
                sp.wait_ge(k_saved[s], count(b, 16, 16))
                if s == "C":
                    sp.wait_ge(scored["B"], count(b, HEADS, HEADS))
                for block in range(4):
                    sp.dma_start(k4[32 * block:32 * block + 32, :, :].bitcast(F32),
                                 k_parts[s][block % 2].rearrange("(p r) t -> r p t", r=2 * DH1)
                                 ).then_inc(spread_k[s], 16)

            def spread_queries(body, step):
                s, b = step[1], body.b
                sp.wait_ge(q_split[s], count(b, 2, 2))
                sp.dma_start(q_parts[:, :, :].rearrange("a (d p) t -> p (a d) t", p=P),
                             q_hl[:, :, :, :].rearrange("p a d t -> p (a d) t")).then_inc(spread_q[s], 16)
                if s == "B":
                    spread_keys(body, step)
                sp.wait_ge(spread_q[s], count(b, 16 * SPREAD["q"], 16))
                for block in range(4):
                    for e in range(2):
                        rows = slice(32 * block + DH1 * e, 32 * block + DH1 * (e + 1))
                        src = q_parts[block // 2].rearrange("(p e r) t -> e r p t", e=2, r=DH1)
                        sp.dma_start(q4[rows, e:HEADS:2, :].bitcast(F32), src[e]).then_inc(spread_q[s], 16)

            sp.dma_start(x_tok[:, :, :], x_d[:, 0]).then_inc(x_in, 16)
            sp.dma_start(c_tok[:, :, :], c_d[:, 0]).then_inc(x_in, 16)
            sp.dma_start(mask_u8[:, :, :], m_d[:, 0]).then_inc(m_in, 16)
            sp.dma_start(qk[:, :, :].bitcast(I32), io["mask_SxS_ik1"].rearrange("(t p) k -> p t k", p=P)
                         ).then_inc(w_in["mask"], 16)
            for w, n in ((wq0, "Wq"), (wk0, "Wk"), (wv0, "Wv")):
                sp.dma_start(w[:, :, :], wide(L0 + n)).then_inc(w_in["proj0"], 16)
            sp.dma_start(wo0[:, :, :], wide(L0 + "Wo")).then_inc(w_in["out0"], 16)
            for n in w1:
                sp.dma_start(w1[n][:, :, :], wide(f"{L1}{n}_w")).then_inc(w_in["attn1"], 16)
            for n in w1o:
                src = io[f"{L1}{n}_w"].rearrange("(o f j d) n -> f j d o n", o=DT, f=2, d=DH1)
                for f in range(2):
                    for j in range(4):
                        r = j * SLOT + f * DH1
                        sp.dma_start(w1o[n][r:r + DH1, :, :], src[f, j]).then_inc(w_in["rows1"], 16)
            for n in ("v", "cv"):
                src = io[f"{L1}{n}_b"].rearrange("(o f j d) -> f j d o", o=DT, f=2, d=DH1)
                for f in range(2):
                    for j in range(4):
                        r = j * SLOT + f * DH1
                        sp.dma_start(col[n][r:r + DH1, :], src[f, j], allow_slow_non_contiguous=True
                                     ).then_inc(w_in["rows1"], 16)
            sp.dma_start(wl1[:, :, :], wide(L1 + "lin1_w")).then_inc(w_in["mlp"], 16)
            sp.dma_start(wl2[:, :, :], wide(L1 + "lin2_w")).then_inc(w_in["mlp"], 16)
            for body in bodies(sp, peel_last=True):
                for step in body.steps:
                    if step[:2] == ("IO", "load"):
                        load(body, step)
                    elif step[:2] == ("IO", "store"):
                        store(body, step)
                    elif step[0] == "DMA":
                        {"save": save_keys, "k": spread_keys, "q": spread_queries}[step[2]](body, step)
            sp.wait_ge(out_done, 16 * BATCH + 16)

        @block.tensor
        def _(pe):
            def wait_bank_free(body, step):
                last = body.earlier(step, 2 if step[1] in DVE_JOBS else 1, ring[step[1]])
                if last:
                    (_, name, i), b = last
                    pe.wait_ge(taken[name], count(b, jobs_of(name), i + 1))

            def product(out, lhs, rhs):
                n = len(lhs)
                for i in range(n):
                    last = nc.tensor.matmul(out, lhs[i], rhs[i], start=i == 0, stop=i == n - 1)
                return last

            def transposes(ps, src):
                for d in range(DT):
                    for t in range(TT):
                        last = nc.tensor.transpose(ps[:, d, t * P:(t + 1) * P],
                                                   src[:, t, d * P:(d + 1) * P], ident[:, :])
                return last

            def columns_out(ps, w, first, src):
                for m in range(2):
                    c = (first + m) * P
                    last = product(ps[:, m, :], [w[:, d, c:c + P] for d in range(DT)],
                                   [src[:, d, :] for d in range(DT)])
                return last

            def tokens_out(ps, src, w):
                n = src.shape[1]
                for t in range(TT):
                    last = product(ps[:, t, :], [src[:, d, t * P:(t + 1) * P] for d in range(n)],
                                   [w[:, d, :] for d in range(n)])
                return last

            def job(body, step):
                _, name, i = step
                b = body.batch(name)
                first = body.before is None
                ps = two(bank_of(body, step))
                wait_bank_free(body, step)
                if name == "xT":
                    pe.wait_ge(x_in, count(b, 32, 32))
                    last = transposes(ps, x_tok)
                elif name == "cT":
                    last = transposes(ps, c_tok)
                elif name in ("q", "k"):
                    pe.wait_ge(taken["xT" if name == "q" else "cT"], count(b, 1, 1))
                    if first:
                        pe.wait_ge(w_in["proj0"], 48)
                    last = columns_out(ps, wq0 if name == "q" else wk0, 2 * i, x_t if name == "q" else c_t)
                elif name == "v":
                    pe.wait_ge(taken["cT"], count(b, 1, 1))
                    half, t = i // TT, i % TT
                    last = product(bank_of(body, step)[:, :], [c_t[:, d, t * P:(t + 1) * P] for d in range(DT)],
                                   [wv0[:, d, half * 512:half * 512 + 512] for d in range(DT)])
                elif name == "kc":
                    if first:
                        pe.wait_ge(w_in["attn1"], 16 * len(w1))
                    last = columns_out(ps, w1["ck"], 0, c_t)
                elif name == "vc":
                    if first:
                        pe.wait_ge(w_in["attn1"], 16 * len(w1))
                    last = tokens_out(ps, c_t, w1["cv"])
                elif name == "wo":
                    pe.wait_ge(ctx_out["A"], count(b, QUADS, QUADS))
                    if first:
                        pe.wait_ge(w_in["out0"], 16)
                    last = tokens_out(ps, k0_ctx, wo0)
                elif name == "x1T":
                    pe.wait_ge(ln_dve["ln0"], count(b, 3, 3))
                    last = transposes(ps, y_a)
                elif name in ("x2T", "x3T"):
                    pe.wait_ge(ln_dve["ln1" if name == "x2T" else "ln2"], count(b, 3, 3))
                    last = transposes(ps, y_b)
                elif name in ("qs", "ks", "qc"):
                    pe.wait_ge(taken["x2T" if name == "qc" else "x1T"], count(b, 1, 1))
                    last = columns_out(ps, w1[{"qs": "q", "ks": "k", "qc": "cq"}[name]], 0, xb_t)
                elif name == "vs":
                    last = tokens_out(ps, xb_t, w1["v"])
                elif name in ("os", "oc"):
                    s = "B" if name == "os" else "C"
                    pe.wait_ge(ctx_out[s], count(b, DT, DT))
                    pe.wait_ge(w_in["rows1"], 16 * 32)
                    last = tokens_out(ps, ctx1, w1o["o" if name == "os" else "co"])
                elif name in ("h", "hd"):
                    pe.wait_ge(taken["x3T"], count(b, 1, 1))
                    pe.wait_ge(w_in["mlp"], 32)
                    last = columns_out(ps, wl1, 2 * i + (FF // P // 2 if name == "hd" else 0), xb_t)
                elif name == "y":
                    pe.wait_ge(taken["h"], count(b, 2, 2))
                    pe.wait_ge(taken["hd"], count(b, 2, 2))
                    last = tokens_out(ps, h_t, wl2)
                last.then_inc(filled[name], 1)

            def scores(body, step):
                _, s, p = step
                b = body.batch(s)
                if s == "A":
                    pe.wait_ge(taken["q"], count(b, 4, p // 2 + 1))
                    pe.wait_ge(taken["k"], count(b, 4, p // 2 + 1))
                else:
                    pe.wait_ge(spread_k[s], count(b, 16 * SPREAD["k"], 16 * SPREAD["k"]))
                    pe.wait_ge(spread_q[s], count(b, 16 * SPREAD["q"], 16 * SPREAD["q"]))
                last_pair = body.earlier(step, 1, lambda x: x[0] == "S")
                for e in range(2):
                    if last_pair:
                        (_, s0, p0), b0 = last_pair
                        pe.wait_ge(masked[s0], count(b0, HEADS, 2 * p0 + e + 1))
                    h = 2 * p + e
                    if s == "A":
                        q, k = qz0[:, h % (4 * Q0_RING), :], k0_ctx[:, p, :]
                    else:
                        q, k = q4[:, h, :], k4[:, p, :]
                    for t in range(TT):
                        last = nc.tensor.matmul(two(ps_s[e])[:, t, :], q[:, t * P:(t + 1) * P], k,
                                                start=True, stop=True)
                    last.then_inc(scored[s], 1)

            def turn(body, step):
                _, s, p = step
                b = body.batch(s)
                src = prob[:, body.slot(s, p, P_RING)]
                pe.wait_ge(normed[s], count(b, PAIRS, p + 1))
                last_pair = body.earlier(step, 1, lambda x: x[0] == "T")
                for e in range(2):
                    if last_pair:
                        (_, s0, p0), b0 = last_pair
                        pe.wait_ge((pt_act, pt_dve)[e][s0], count(b0, PAIRS, p0 + 1))
                    for kt in range(TT):
                        for qt in range(TT):
                            last = nc.tensor.transpose(two(ps_t[e])[:, kt, qt * P:(qt + 1) * P],
                                                       src[:, e, qt, kt * P:(kt + 1) * P], ident[:, :])
                    last.then_inc(turned[s], 1)

            def weigh(body, step):
                _, s, quad = step
                b = body.batch(s)
                pe.wait_ge(pt_act[s], count(b, PAIRS, 2 * quad + 2))
                pe.wait_ge(pt_dve[s], count(b, PAIRS, 2 * quad + 2))
                if s == "A":
                    pe.wait_ge(taken["v"], count(b, 4, 2 * (quad // 2) + 2))
                else:
                    pe.wait_ge(taken["vs" if s == "B" else "vc"], count(b, 1, 1))
                last_quad = body.earlier(step, 1, lambda x: x[0] == "AV")
                if last_quad and (s == "A" or quad % 2 == 0):
                    (_, s0, q0), b0 = last_quad
                    pe.wait_ge(ctx_out[s0], count(b0, CTX_OUTS[s0], q0 + 1 if s0 == "A" else q0 // 2 + 1))
                if s == "A":
                    for j in range(2):
                        pt = prob_t[:, body.slot(s, 2 * quad + j, PT_RING)]
                        for kt in range(TT):
                            for e in range(2):
                                h = 4 * quad + 2 * j + e
                                last = nc.tensor.matmul(two(ps_av)[e * DH0:(e + 1) * DH0, j, :],
                                                        v0[:, kt, h * DH0:(h + 1) * DH0], pt[:, e, kt, :],
                                                        start=kt == 0, stop=kt == TT - 1)
                else:
                    for kt in range(TT):
                        for j in range(4):
                            h = 4 * quad + j
                            pt = prob_t[:, body.slot(s, 2 * quad + j // 2, PT_RING)]
                            last = nc.tensor.matmul(ps_av[j * SLOT:(j + 1) * SLOT, 0:TOK],
                                                    v1[s][:, kt, h, :], pt[:, j % 2, kt, :],
                                                    start=kt == 0 and quad % 2 == 0,
                                                    stop=kt == TT - 1 and quad % 2 == 1,
                                                    tile_position=(0, j * SLOT))
                last.then_inc(weighed[s], 1)

            pe.wait_ge(const_ready, 1)
            for body in bodies(pe):
                for step in body.steps:
                    {"J": job, "S": scores, "T": turn, "AV": weigh}.get(step[0], lambda *_: None)(body, step)

        @block.scalar
        def _(act):
            act.dma_start(col["bq0"][:, :], column(L0 + "bq"), allow_slow_non_contiguous=True).then_inc(w_in["small"], 16)
            act.dma_start(col["bk0"][:, :], column(L0 + "bk"), allow_slow_non_contiguous=True).then_inc(w_in["small"], 16)
            act.dma_start(col["bv0"][:, :], column(L0 + "bv"), allow_slow_non_contiguous=True
                          ).then_inc(w_in["small"], 16)
            for n, src in (("g0", L0 + "gamma"), ("b0", L0 + "beta"), ("g1", L1 + "ln1_g"),
                           ("b1", L1 + "ln1_b"), ("g2", L1 + "ln2_g"), ("b2", L1 + "ln2_b")):
                act.dma_start(col[n][:, :], column(src), allow_slow_non_contiguous=True
                              ).then_inc(w_in["small"], 16)
            for n in ("q", "k", "cq", "ck"):
                act.dma_start(col[n][:, :], column(f"{L1}{n}_b"), allow_slow_non_contiguous=True).then_inc(w_in["small"], 16)
            act.dma_start(col["l1"][:, :], column(L1 + "lin1_b"), allow_slow_non_contiguous=True).then_inc(w_in["small"], 16)
            for n, src in (("bo0", L0 + "bo"),
                           ("g0", L0 + "gamma"), ("b0", L0 + "beta"), ("g1", L1 + "ln1_g"),
                           ("b1", L1 + "ln1_b"), ("g2", L1 + "ln2_g"), ("b2", L1 + "ln2_b"),
                           ("g3", L1 + "ln3_g"), ("b3", L1 + "ln3_b")):
                act.dma_start(row[n][:, :], io[src].partition_broadcast(P)).then_inc(w_in["small"], 16)
            for n, src in (("o", L1 + "o_b"), ("co", L1 + "co_b"), ("l2", L1 + "lin2_b")):
                act.dma_start(landing[n], io[src].partition_broadcast(P)).then_inc(w_in["small"], 16)
            act.wait_ge(w_in["small"], 16 * small)

            def job(body, step):
                _, name, i = step
                b = body.batch(name)
                if name not in ACT_JOBS:
                    return
                ps = two(ps_ga)
                act.wait_ge(filled[name], count(b, jobs_of(name), i + 1))
                if name in ("xT", "cT"):
                    nc.scalar.activation((x_t if name == "xT" else c_t)[:, :, :], ps,
                                         ACT.Copy).then_inc(taken[name], 1)
                    return
                if name in ("vs", "vc"):
                    v = v1["B" if name == "vs" else "C"][:, :, :, :]
                    for f in range(2):
                        last = nc.scalar.activation(
                            v.rearrange("p t (o f j) d -> p (t o) f j d", f=2, j=4)[:, :, f, :, DH1 * f:DH1 * (f + 1)],
                            ps.rearrange("p t (o f j d) -> p (t o) f j d", f=2, j=4, d=DH1)[:, :, f], ACT.Copy)
                    last.then_inc(taken[name], 1)
                    return
                if name in ("x1T", "x2T", "x3T"):
                    n = str(int(name[1]) - 1)
                    for d in range(DT):
                        last = nc.scalar.activation(xb_t[:, d, :], ps[:, d, :], ACT.Identity,
                                                    bias=col["b" + n][:, d:d + 1],
                                                    scale=col["g" + n][:, d:d + 1])
                    last.then_inc(taken[name], 1)
                    return
                out, bias = (k0_ctx, col["bk0"]) if name == "k" else (h_t, col["l1"])
                for m in range(2):
                    c = 2 * i + m
                    last = nc.scalar.activation(out[:, c, :], ps[:, m, :],
                                                ACT.Relu if name == "h" else ACT.Identity,
                                                bias=bias[:, c:c + 1])
                last.then_inc(taken[name], 1)

            def exps(body, step):
                _, s, p = step
                b = body.batch(s)
                slot = body.slot(s, p, P_RING)
                for e in range(2):
                    act.wait_ge(masked[s], count(b, HEADS, 2 * p + e + 1))
                    for t in range(TT):
                        tile = prob[:, slot, e, t, :]
                        last = nc.scalar.activation(tile, tile, ACT.Exp, bias=ext[:, slot, e, t:t + 1],
                                                    scale=-1.0, accum_out=sums[:, slot, e, t:t + 1])
                last.then_inc(exped[s], 1)

            def evac_turned(body, step):
                _, s, p = step
                act.wait_ge(turned[s], count(body.batch(s), HEADS, 2 * p + 1))
                nc.scalar.activation(prob_t[:, body.slot(s, p, PT_RING), 0], two(ps_t[0]),
                                     ACT.Copy).then_inc(pt_act[s], 1)

            def evac_weighed(body, step):
                _, s, quad = step
                if s != "A" and quad % 2 == 0:
                    return
                act.wait_ge(weighed[s], count(body.batch(s), QUADS, quad + 1))
                if s == "A":
                    for j in range(2):
                        c = 2 * quad + j
                        last = nc.scalar.activation(k0_ctx[:, c, :], two(ps_av)[:, j, :], ACT.Identity,
                                                    bias=col["bv0"][:, c:c + 1])
                    last.then_inc(ctx_out[s], 1)
                else:
                    act.wait_ge(w_in["rows1"], 16 * 32)
                    o = quad // 2
                    bias = col["v" if s == "B" else "cv"][:, o:o + 1]
                    nc.scalar.activation(ctx1[:, o, :], ps_av[:, 0:TOK], ACT.Identity, bias=bias
                                         ).then_inc(ctx_out[s], 1)

            for body in bodies(act):
                for step in body.steps:
                    {"J": job, "S": exps, "T": evac_turned, "AV": evac_weighed}.get(
                        step[0], lambda *_: None)(body, step)

        @block.vector
        def _(dve):
            dve.wait_ge(w_in["small"], 16 * small)
            for n in "BC":
                nc.vector.memset(v1[n][:, :, :, :], 0.0)
            nc.vector.memset(qz0[DH0:P, 0:4 * Q0_RING:2, :], 0.0)
            nc.vector.memset(qz0[0:DH0, 1:4 * Q0_RING:2, :], 0.0)
            nc.vector.memset(q4[:, :, :].bitcast(F32), 0.0)
            for n, bias in (("b0", "o"), ("b1", "co"), ("b2", "l2")):
                nc.vector.tensor_tensor(row[n][:, :], row[n][:, :], landing[bias], ALU.add)
            nc.vector.memset(eps[:, :], EPS)
            nc.vector.memset(minus_half[:, :], -0.5)
            nc.vector.memset(zero[:, :], 0.0).then_inc(out_done, 16)
            dve.wait_ge(out_done, 16)
            nc.vector.memset(mv["a"][:, :, :], 0.0).then_inc(dve_const, 1)
            dve.wait_ge(w_in["mask"], 16)
            nc.vector.tensor_scalar(mask_b[:, :, :], qk[:, :, :].bitcast(I32), 0.0, -BIG,
                                    ALU.not_equal, ALU.mult).then_inc(mask_b_ready, 1)
            dve.wait_ge(mask_b_ready, 1)

            def held(value):
                return value if isinstance(value, int) else dve.to_reg(value)

            def job(body, step):
                _, name, i = step
                b = body.batch(name)
                if name == "cT":
                    dve.wait_ge(m_in, count(b, 16, 16))
                    nc.vector.tensor_scalar(mask_a[:, :, :], mask_u8[:, :, :], 0.0, -BIG,
                                            ALU.not_equal, ALU.mult).then_inc(mask_read, 1)
                if name not in DVE_JOBS:
                    return
                bank = bank_of(body, step)
                ps = two(bank)
                dve.wait_ge(filled[name], count(b, jobs_of(name), i + 1))
                if name == "q":
                    for e in range(2):
                        r = slice(e * DH0, (e + 1) * DH0)
                        first = 4 * (i % Q0_RING) + e
                        bias = col["bq0"][r, 2 * i:2 * i + 2].unsqueeze(2).to_broadcast([DH0, 2, TOK])
                        last = nc.vector.tensor_tensor(qz0[r, first:first + 3:2, :], ps[r], bias, ALU.add)
                    last.then_inc(taken[name], 1)
                elif name == "v":
                    half, t = i // TT, i % TT
                    nc.vector.tensor_copy(v0[:, t, half * 512:half * 512 + 512], bank[:, :]
                                          ).then_inc(taken[name], 1)
                elif name in ("qs", "qc", "ks", "kc"):
                    s = "B" if name[1] == "s" else "C"
                    bias = col[{"qs": "q", "qc": "cq", "ks": "k", "kc": "ck"}[name]]
                    parts, done = (q_hl, q_split[s]) if name[0] == "q" else (k_hl, k_split[s])
                    if name == "qs":
                        dve.wait_ge(k_split["B"], count(b, 2, 2))
                    elif name == "ks":
                        dve.wait_ge(k_split["C"], count(b, 2, 2))
                    elif name == "qc":
                        dve.wait_ge(q_split["B"], count(b, 2, 2))
                    elif body.b is not None:
                        dve.wait_ge(q_split["C"], count(body.b, 2, 2))
                    nc.vector.tensor_tensor(qk[:, :, :], ps, bias[:, :].unsqueeze(2).to_broadcast([P, DT, TOK]),
                                            ALU.add).then_inc(taken[name], 1)
                    if name == "ks":
                        dve.wait_ge(k_saved["C"], count(b, 16, 16))
                    elif name == "kc" and body.b is not None:
                        dve.wait_ge(k_saved["B"], count(body.b, 16, 16))
                    dve.wait_ge(taken[name], count(b, 1, 1))
                    nc.vector.tensor_copy(parts[:, 0].bitcast(F32R), qk[:, :, :]).then_inc(done, 1)
                    dve.wait_ge(done, count(b, 2, 1))
                    nc.vector.tensor_tensor(parts[:, 1].bitcast(F32R), qk[:, :, :], parts[:, 0],
                                            ALU.subtract).then_inc(done, 1)
                elif name == "hd":
                    for m in range(2):
                        c = FF // P // 2 + 2 * i + m
                        last = nc.vector.tensor_scalar(h_t[:, c, :], ps[:, m, :], col["l1"][:, c:c + 1],
                                                       0.0, ALU.add, ALU.max)
                    last.then_inc(taken[name], 1)
                else:
                    residual(name, b, ps)

            def residual(name, b, ps):
                ln = LN_AFTER[name]
                k, y, res = ("a", y_a, res_a) if ln == "ln0" else ("b", y_b, {"ln1": res_ab}.get(ln, res_b))
                before = {"ln0": "x", "ln1": "ln0", "ln2": "ln1", "ln3": "ln2"}[ln]
                n = 1 if before == "x" else 2
                dve.wait_ge(res_ready[before], count(b, n, n))
                nc.vector.tensor_tensor(y[:, :, :], ps, res[:, :, :], ALU.add).then_inc(taken[name], 1)
                dve.wait_ge(taken[name], count(b, 1, 1))
                for t in range(TT):
                    last = nc.vector.bn_stats(stats[k][:, t, :], y[:, t, :])
                last.then_inc(ln_dve[ln], 1)
                value = held(count(b, LN_STEPS[ln], 1))
                dve.wait_ge(dve_const, 1)
                dve.wait_ge(ln_dve[ln], value)
                for t in range(TT):
                    last = nc.vector.bn_aggr(mv[k][:, t, :], stats[k][:, t, :])
                last.then_inc(ln_dve[ln], 1)

            def layer_norm(body, step):
                ln = step[1]
                b = body.a if ln == "ln0" else body.b
                k, y = ("a", y_a) if ln == "ln0" else ("b", y_b)
                dve.wait_ge(ln_rstd[ln], count(b, 2, 2))
                for t in range(TT):
                    last = nc.vector.tensor_scalar(y[:, t, :], y[:, t, :], mv[k][:, t, 0:1],
                                                   rstd[k][:, t:t + 1], ALU.subtract, ALU.mult)
                last.then_inc(ln_dve[ln], 1)
                if ln != "ln3":
                    return
                g, beta = (row[n][:, :].unsqueeze(1).to_broadcast([P, TT, D]) for n in LN_ROWS[ln])
                dve.wait_ge(ln_dve[ln], count(b, 5, 3))
                nc.vector.tensor_tensor(y[:, :, :], y[:, :, :], g, ALU.mult).then_inc(ln_dve[ln], 1)
                dve.wait_ge(ln_dve[ln], count(b, 5, 4))
                dve.wait_ge(out_done, count(b, 16, 16))
                nc.vector.tensor_tensor(y_out[:, :, :], y[:, :, :], beta, ALU.add).then_inc(ln_dve[ln], 1)

            def extremes(body, step):
                _, s, p = step
                b = body.batch(s)
                slot = body.slot(s, p, P_RING)
                if s == "A" and p == 0:
                    dve.wait_ge(mask_read, count(b, 1, 1))
                for e in range(2):
                    value = held(count(b, HEADS, 2 * p + e + 1))
                    dve.wait_ge(dve_const, 1)
                    dve.wait_ge(scored[s], value)
                    for t in range(TT):
                        mask = {"A": mask_a[:, t, :], "B": mask_b[:, t, :],
                                "C": zero[:, :].to_broadcast([P, TOK])}[s]
                        last = nc.vector.tensor_tensor_reduce(
                            out=prob[:, slot, e, t, :], in0=two(ps_s[e])[:, t, :], in1=mask,
                            scale=-SCALE[s], scalar=BIG, op0=ALU.add, op1=ALU.min,
                            accum_out=ext[:, slot, e, t:t + 1])
                    last.then_inc(masked[s], 1)

            def reciprocals(body, step):
                _, s, p = step
                slot = body.slot(s, p, P_RING)
                dve.wait_ge(exped[s], count(body.batch(s), PAIRS, p + 1))
                nc.vector.reciprocal(recip[:, slot], sums[:, slot]).then_inc(recipd[s], 1)

            def evac_turned(body, step):
                _, s, p = step
                dve.wait_ge(turned[s], count(body.batch(s), HEADS, 2 * p + 2))
                nc.vector.tensor_copy(prob_t[:, body.slot(s, p, PT_RING), 1], two(ps_t[1])).then_inc(pt_dve[s], 1)

            for body in bodies(dve):
                for step in body.steps:
                    {"J": job, "LN": layer_norm, "S": extremes, "R": reciprocals, "T": evac_turned}.get(
                        step[0], lambda *_: None)(body, step)

        @block.gpsimd
        def _(pool):
            nc.gpsimd.memset(ident[:, :], 1.0).then_inc(pool_step, 1)
            pool.wait_ge(pool_step, 1)
            nc.gpsimd.affine_select(out=ident[:, :], in_=ident[:, :], compare_op=ALU.is_equal, fill=0.0,
                                    base=0, pattern=[[-1, P]], channel_multiplier=1).then_inc(const_ready, 1)
            pool.wait_ge(w_in["small"], 16 * small)
            pool.wait_ge(dve_const, 1)

            def job(body, step):
                _, name, i = step
                b = body.batch(name)
                if name == "xT":
                    pool.wait_ge(x_in, count(b, 32, 32))
                    nc.gpsimd.tensor_tensor(res_a[:, :, :], x_tok[:, :, :],
                                            row["bo0"][:, :].unsqueeze(1).to_broadcast([P, TT, D]),
                                            ALU.add).then_inc(res_ready["x"], 1)
                elif name in LN_AFTER:
                    ln = LN_AFTER[name]
                    k = "a" if ln == "ln0" else "b"
                    pool.wait_ge(ln_dve[ln], count(b, LN_STEPS[ln], 2))
                    nc.gpsimd.tensor_tensor(var_eps[k][:, :], mv[k][:, :, 1], eps[:, :],
                                            ALU.add).then_inc(ln_rstd[ln], 1)
                    pool.wait_ge(ln_rstd[ln], count(b, 2, 1))
                    nc.gpsimd.tensor_tensor(rstd[k][:, :], var_eps[k][:, :], minus_half[:, :],
                                            ALU.pow).then_inc(ln_rstd[ln], 1)

            def next_residual(body, step):
                ln = step[1]
                if ln == "ln3":
                    return
                b = body.a if ln == "ln0" else body.b
                y, out = (y_a, res_ab) if ln == "ln0" else (y_b, res_b)
                g, beta = (row[n][:, :].unsqueeze(1).to_broadcast([P, TT, D]) for n in LN_ROWS[ln])
                pool.wait_ge(ln_dve[ln], count(b, 3, 3))
                nc.gpsimd.tensor_tensor(out[:, :, :], y[:, :, :], g, ALU.mult).then_inc(res_ready[ln], 1)
                pool.wait_ge(res_ready[ln], count(b, 2, 1))
                nc.gpsimd.tensor_tensor(out[:, :, :], out[:, :, :], beta, ALU.add).then_inc(res_ready[ln], 1)

            def normalize(body, step):
                _, s, p = step
                slot = body.slot(s, p, P_RING)
                pool.wait_ge(recipd[s], count(body.batch(s), PAIRS, p + 1))
                flat = prob[:, slot].rearrange("p e t k -> p (e t) k")
                nc.gpsimd.tensor_tensor(flat, flat,
                                        recip[:, slot].rearrange("p e t -> p (e t)").unsqueeze(2)
                                        .to_broadcast([P, 2 * TT, TOK]), ALU.mult).then_inc(normed[s], 1)

            for body in bodies(pool):
                for step in body.steps:
                    {"J": job, "LN": next_residual, "R": normalize}.get(
                        step[0], lambda *_: None)(body, step)


_OUT = (BATCH, TOK, D)


def kernel(**inputs):
    import concourse.bacc as bacc
    from concourse.bass_utils import run_bass_kernel_spmd

    nc = bacc.Bacc("TRN2", target_bir_lowering=False, num_devices=1)
    arrays = {n: np.ascontiguousarray(a) for n, a in inputs.items()}
    io = {n: nc.dram_tensor(n, a.shape, mybir.dt.from_np(a.dtype), kind="ExternalInput").ap()
          for n, a in arrays.items()}
    io["out"] = nc.dram_tensor("out", _OUT, F32, kind="ExternalOutput").ap()
    program(nc, io)
    return run_bass_kernel_spmd(nc, [arrays], core_ids=[0]).results[0]["out"]
```

```python
from contextlib import ExitStack

import numpy as np

import concourse.bass as bass
from concourse import mybir

ALU = mybir.AluOpType
ACT = mybir.ActivationFunctionType
F32 = mybir.dt.float32
F32R = mybir.dt.float32r
BF16 = mybir.dt.bfloat16
I32 = mybir.dt.int32
U8 = mybir.dt.uint8

P = 128
BATCH, TOK, D = 16, 256, 256
TT, DT = TOK // P, D // P
HEADS = 16
PAIRS, QUADS = HEADS // 2, HEADS // 4
DH0, DH1 = 64, D // HEADS
INNER = HEADS * DH0
FF = 1024
SLOT = 32
EPS = 1e-5
BIG = 2.0 ** 127
SCALE = {"A": DH0 ** -0.5, "B": DH1 ** -0.5, "C": DH1 ** -0.5}

P_RING, PT_RING = 4, 3
LAG_R = 1

DVE_JOBS = {"xT": 1, "cT": 1, "q": 4, "v": 4, "kc": 1, "wo": 1,
            "qs": 1, "ks": 1, "vs": 1, "os": 1, "qc": 1, "oc": 1, "hd": 1, "y": 1}
ACT_JOBS = {"k": 4, "vc": 1, "x1T": 1, "x2T": 1, "x3T": 1, "h": 3}
STREAM_A = {"A", "q", "v", "vc", "wo", "xT", "cT", "k", "kc", "load"}
STREAM_M = {"x3T", "h", "hd", "y", "ln3", "store"}
LN_STEPS = {"ln0": 3, "ln1": 3, "ln2": 3, "ln3": 5}
Q0_RING = 2


def schedule(a, b, m):
    job = lambda name, i=0: ("J", name, i)
    pairs = lambda name, *ps: [(name, p) for p in ps]
    steps = []

    def attend(order, after, late=None, drained=((), (), ())):
        n, late = len(order), late or {}
        turn_at = [g + (3 if all(o[0] != "A" for o in order[g:g + 4]) and g + 4 <= n else 2)
                   for g in range(n)]
        waiting = []
        for g in range(n + 3):
            if g < n:
                steps.append(("S",) + order[g])
            if 0 <= g - LAG_R < n:
                steps.append(("R",) + order[g - LAG_R])
            if g < n and order[g][0] == "A":
                steps.extend(waiting)
                waiting = []
            steps.extend(after.get(order[g], []) if g < n else drained[g - n])
            if g not in turn_at:
                steps.extend(waiting)
                waiting = []
            turned = []
            for i in range(n):
                if turn_at[i] == g:
                    name, p = order[i]
                    steps.append(("T", name, p))
                    steps.extend(waiting)
                    waiting = []
                    if p % 2:
                        turned.append(("AV", name, p // 2))
            waiting += turned
            steps.extend(late.get(order[g], []) if g < n else [])

    ks, qs = [job("ks"), ("DMA", "B", "save")], [job("qs"), ("DMA", "B", "q")]
    kc, k_spread = [job("kc"), ("DMA", "C", "save")], ("DMA", "C", "k")
    qc = [job("qc"), ("DMA", "C", "q")]
    x3, h, hd, y, ends_mlp = [], [[]] * 3, [], [], []
    if m:
        x3, h, hd, y = [job("x3T")], [[job("h", i)] for i in range(3)], [job("hd")], [job("y")]
        ends_mlp = [("LN", "ln3", 0), ("IO", "store", 0)]

    if a and b:
        steps += x3 + [job("xT"), job("cT"), ("IO", "load", 0)] + h[0]
        steps += [("LN", "ln0", 0), job("q", 0), job("k", 0), job("v", 0), job("x1T"), job("v", 1)]
        steps += ks + qs + [job("vs"), job("k", 1)]
        attend(pairs("A", 0, 1) + pairs("B", *range(8)) + pairs("A", 2, 3, 4, 5),
               {("A", 0): [job("q", 1)], ("A", 1): h[1], ("B", 2): [job("q", 2)], ("B", 3): hd,
                ("B", 4): [job("k", 2)], ("B", 6): h[2], ("A", 2): [k_spread],
                ("A", 5): [("LN", "ln1", 0)]},
               {("A", 4): [job("os")]},
               ([job("v", 2), job("x2T")], qc + y, [job("q", 3)]))
        attend(pairs("C", *range(8)) + pairs("A", 6, 7),
               {("C", 4): [job("k", 3)]},
               {}, ([job("v", 3)], ends_mlp, [job("oc"), job("vc")]))
        steps += kc + [("LN", "ln2", 0), job("wo")]
    elif a:
        steps += [job("xT"), job("cT"), ("IO", "load", 0), job("q", 0), job("k", 0), job("q", 1),
                  job("k", 1)] + [job("v", i) for i in range(4)] + [job("k", 2), job("k", 3)]
        attend(pairs("A", *range(8)), {("A", 1): [job("q", 2)], ("A", 3): [job("q", 3)]})
        steps += [job("vc")] + kc + [job("wo")]
    elif b:
        steps += x3 + [("LN", "ln0", 0), job("x1T")] + ks + h[0] + qs + h[1] + [job("vs")]
        attend(pairs("B", *range(8)), {("B", 2): hd, ("B", 4): h[2]})
        steps += [k_spread, job("os"), ("LN", "ln1", 0), job("x2T")] + qc + y
        attend(pairs("C", *range(8)), {("C", 3): ends_mlp})
        steps += [job("oc"), ("LN", "ln2", 0)]
    else:
        steps += x3 + hd + h[0] + h[1] + h[2] + y + ends_mlp
    return steps


class Body:

    def __init__(self, a, b, m, before=None):
        self.a, self.b, self.m, self.before = a, b, m, before
        self.streams = [x is not None for x in (a, b, m)]
        self.steps = schedule(*self.streams)
        self.pairs = [s[1:] for s in self.steps if s[0] == "S"]

    def batch(self, name):
        return self.a if name in STREAM_A else self.m if name in STREAM_M else self.b

    def slot(self, name, p, ring):
        return self.pairs.index((name, p)) % ring

    def earlier(self, step, back, same):
        mine = [s for s in self.steps if same(s)]
        i = mine.index(step) - back
        if i >= 0:
            return mine[i], self.batch(mine[i][1])
        if self.before is None:
            return None
        last = [s for s in self.before.steps if same(s)][i]
        if all(self.streams):
            assert last[1] in STREAM_A and last == mine[i]
        return last, self.before.batch(last[1])


def program(nc, io):
    with ExitStack() as ctx:
        def sb(name, shape, dt=F32):
            return ctx.enter_context(nc.sbuf_tensor(name, shape, dt))

        def sem(name):
            return ctx.enter_context(nc.semaphore(name))

        wq0, wk0, wv0 = (sb(n, [P, DT, INNER]) for n in ("wq0", "wk0", "wv0"))
        wo0 = sb("wo0", [P, INNER // P, D])
        w1 = {n: sb("w_" + n, [P, DT, D]) for n in ("q", "k", "v", "cq", "ck", "cv")}
        w1o = {n: sb("w_" + n, [P, DT, D]) for n in ("o", "co")}
        wl1 = sb("wl1", [P, DT, FF])
        wl2 = sb("wl2", [P, FF // P, D])
        col = {n: sb("col_" + n, [P, k]) for n, k in
               (("bq0", PAIRS), ("bk0", PAIRS), ("bv0", PAIRS), ("q", DT), ("k", DT), ("cq", DT),
                ("ck", DT), ("v", DT), ("cv", DT), ("l1", FF // P), ("g0", DT), ("b0", DT),
                ("g1", DT), ("b1", DT), ("g2", DT), ("b2", DT))}
        row = {n: sb("row_" + n, [P, D]) for n in
               ("bo0", "g0", "b0", "g1", "b1", "g2", "b2", "g3", "b3")}
        ident = sb("ident", [P, P])
        zero = sb("zero", [P, 1])
        minus_half, eps = sb("minus_half", [P, TT]), sb("eps", [P, TT])

        x_tok, c_tok = sb("x_tok", [P, TT, D]), sb("c_tok", [P, TT, D])
        mask_u8 = sb("mask_u8", [P, TT, TOK], U8)
        mask_a = sb("mask_a", [P, TT, TOK], BF16)
        mask_b = sb("mask_b", [P, TT, TOK], BF16)
        x_t, c_t = sb("x_t", [P, DT, TOK]), sb("c_t", [P, DT, TOK])
        qz0 = sb("qz0", [P, Q0_RING * HEADS // 4, TOK])
        k0_ctx = sb("k0_ctx", [P, PAIRS, TOK])
        v0 = sb("v0", [P, TT, INNER])
        prob = sb("prob", [P, P_RING, 2, TT, TOK])
        prob_t = sb("prob_t", [P, PT_RING, 2, TT, TOK])
        ext, sums, recip = (sb(n, [P, P_RING, 2, TT]) for n in ("ext", "sums", "recip"))
        qk = sb("qk", [P, DT, TOK])
        k_hl, q_hl = sb("k_hl", [P, 2, DT, TOK]), sb("q_hl", [P, 2, DT, TOK])
        k4 = sb("k4", [P, PAIRS, TOK], F32R)
        q4 = sb("q4", [P, HEADS, TOK], F32R)
        h_t = sb("h_t", [P, FF // P, TOK])
        v1 = {"B": sb("v_self", [P, TT, HEADS, SLOT]), "C": sb("v_cross", [P, TT, HEADS, SLOT])}
        ctx1 = sb("ctx1", [P, DT, TOK])
        y_a, y_b = sb("y_a", [P, TT, D]), sb("y_b", [P, TT, D])
        res_a, res_ab, res_b, res_m = (sb(n, [P, TT, D]) for n in ("res_a", "res_ab", "res_b", "res_m"))
        y_out = sb("y_out", [P, TT, D])
        xb_t = sb("xb_t", [P, DT, TOK])
        x_mlp_t = sb("x_mlp_t", [P, DT, TOK])
        stats = {s: sb("stats_" + s, [P, TT, 6]) for s in "abm"}
        mv = {s: sb("mv_" + s, [P, TT, 2]) for s in "abm"}
        rstd = {s: sb("rstd_" + s, [P, TT]) for s in "abm"}
        var_eps = {s: sb("var_eps_" + s, [P, TT]) for s in "abm"}

        landing = {n: h_t[:, DT + i, :] for i, n in enumerate(("o", "co", "l2"))}

        bank = lambda n: ctx.enter_context(nc.psum_tensor(n, [P, 512], F32))
        ps_s = [bank("ps_s0"), bank("ps_s1")]
        ps_t = [bank("ps_t0"), bank("ps_t1")]
        ps_av = bank("ps_av")
        ps_gd = [bank("ps_gd0"), bank("ps_gd1")]
        ps_ga = bank("ps_ga")
        two = lambda t: t[:, :].rearrange("p (a n) -> p a n", a=2)

        w_in = {n: sem("w_in_" + n) for n in ("q0", "k0", "v0", "bias0", "out0", "attn1", "rows1",
                                              "mlp", "small", "mask")}
        x_in, m_in = sem("x_in"), sem("m_in")
        out_done = sem("out_done")
        ident_ready = sem("ident_ready")
        dve_const = sem("dve_const")
        zeros_ready = sem("zeros_ready")
        mask_read = sem("mask_read")
        mask_b_ready = sem("mask_b_ready")
        pool_step = sem("pool_step")
        att = "ABC"
        small = len(col) - 5 + len(row) + 3
        SPREAD = {"k": 4, "q": 8}
        scored = {s: sem("scored_" + s) for s in att}
        masked = {s: sem("masked_" + s) for s in att}
        exped = {s: sem("exped_" + s) for s in att}
        recipd = {s: sem("recipd_" + s) for s in att}
        normed = {s: sem("normed_" + s) for s in att}
        turned = {s: sem("turned_" + s) for s in att}
        pt_act = {s: sem("pt_act_" + s) for s in att}
        pt_dve = {s: sem("pt_dve_" + s) for s in att}
        weighed = {s: sem("weighed_" + s) for s in att}
        ctx_out = {s: sem("ctx_out_" + s) for s in att}
        CTX_OUTS = {"A": QUADS, "B": DT, "C": DT}
        filled = {n: sem("filled_" + n) for n in {**DVE_JOBS, **ACT_JOBS}}
        taken = {n: sem("taken_" + n) for n in {**DVE_JOBS, **ACT_JOBS}}
        q_split = {s: sem("q_split_" + s) for s in "BC"}
        k_split = {s: sem("k_split_" + s) for s in "BC"}
        q_saved = {s: [sem(f"q_saved_{part}_{s}") for part in ("high", "low")] for s in "BC"}
        k_saved = {s: sem("k_saved_" + s) for s in "BC"}
        spread_k = {s: sem("spread_k_" + s) for s in "BC"}
        spread_q = {s: sem("spread_q_" + s) for s in "BC"}
        k_parts = {s: nc.dram_tensor("k_parts_" + s, (2, D, TOK), F32) for s in "BC"}
        q_parts = nc.dram_tensor("q_parts", (2, D, TOK), F32)
        lns = ("ln0", "ln1", "ln2", "ln3")
        ln_dve = {n: sem("dve_" + n) for n in lns}
        ln_rstd = {n: sem("rstd_" + n) for n in lns}
        res_ready = {n: sem("res_" + n) for n in ("x", "ln0", "ln1", "ln2")}

        tok_view = lambda t: t.rearrange("b (t p) d -> p b t d", p=P)
        x_d, c_d, m_d, o_d = (tok_view(io[n]) for n in
                              ("x", "ctx_1024", "mask_BxSxS2_bf0", "out"))
        wide = lambda n: io[n].rearrange("(k p) n -> p k n", p=P)
        column = lambda n: io[n].rearrange("(k p) -> p k", p=P)
        L0, L1 = "L0_xattn_", "L1_xattn_"

        def count(b, per, n):
            return b * per + n

        def jobs_of(name):
            return DVE_JOBS.get(name) or ACT_JOBS[name]

        ring = {**{n: (lambda s: s[0] == "J" and s[1] in DVE_JOBS) for n in DVE_JOBS},
                **{n: (lambda s: s[0] == "J" and s[1] in ACT_JOBS) for n in ACT_JOBS}}

        def bank_of(body, step):
            if step[1] in ACT_JOBS:
                return ps_ga
            mine = [s for s in body.steps if ring[step[1]](s)]
            return ps_gd[mine.index(step) % 2]

        LN_BUFFERS = {"ln0": ("a", y_a, res_a), "ln1": ("b", y_b, res_ab), "ln2": ("b", y_b, res_b),
                      "ln3": ("m", y_out, res_m)}
        LN_AFTER = {"wo": "ln0", "os": "ln1", "oc": "ln2", "y": "ln3"}
        LN_ROWS = {"ln0": ("g0", "b0"), "ln1": ("g1", "b1"), "ln2": ("g2", "b2"), "ln3": ("g3", "b3")}

        def bodies(eng, peel_last=False):
            first = Body(0, None, None)
            yield first
            yield Body(1, 0, None, first)
            with eng.Fori(0, BATCH - 2 - peel_last) as it:
                yield Body(it + 2, it + 1, it, Body(it + 1, it, None))
            last_a = Body(BATCH - 1, BATCH - 2, BATCH - 3, Body(BATCH - 2, BATCH - 3, None))
            if peel_last:
                yield last_a
            last_b = Body(None, BATCH - 1, BATCH - 2, last_a)
            yield last_b
            yield Body(None, None, BATCH - 1, last_b)

        block = ctx.enter_context(nc.Block())

        @block.sync
        def _(sp):
            def load(body, step):
                b = body.a
                if isinstance(b, int) and b == BATCH - 1:
                    return
                sp.wait_ge(filled["cT"], count(b, 1, 1))
                sp.wait_ge(res_ready["x"], count(b, 1, 1))
                sp.dma_start(x_tok[:, :, :].unsqueeze(1), x_d[:, bass.ds(b + 1, 1)]).then_inc(x_in, 16)
                sp.dma_start(c_tok[:, :, :].unsqueeze(1), c_d[:, bass.ds(b + 1, 1)]).then_inc(x_in, 16)
                sp.wait_ge(mask_read, count(b, 1, 1))
                sp.dma_start(mask_u8[:, :, :].unsqueeze(1), m_d[:, bass.ds(b + 1, 1)]).then_inc(m_in, 16)

            def store(body, step):
                b = body.m
                sp.wait_ge(ln_dve["ln3"], count(b, 5, 5))
                sp.dma_start(o_d[:, bass.ds(b, 1)], y_out[:, :, :].unsqueeze(1)).then_inc(out_done, 16)

            def save_keys(body, step):
                s = step[1]
                b = body.b if s == "B" else body.a
                sp.wait_ge(k_split[s], count(b, 2, 2))
                if body.b is not None:
                    if s == "C":
                        sp.wait_ge(spread_k["C"], count(body.b, 16 * SPREAD["k"], 16 * SPREAD["k"]))
                sp.dma_start(k_parts[s][:, :, :].rearrange("a (d p) t -> p (a d) t", p=P),
                             k_hl[:, :, :, :].rearrange("p a d t -> p (a d) t")).then_inc(k_saved[s], 16)

            def spread_keys(body, step):
                s, b = step[1], body.b
                sp.wait_ge(k_saved[s], count(b, 16, 16))
                if s == "C":
                    sp.wait_ge(scored["B"], count(b, HEADS, HEADS))
                for block in range(4):
                    sp.dma_start(k4[32 * block:32 * block + 32, :, :].bitcast(F32),
                                 k_parts[s][block % 2].rearrange("(p r) t -> r p t", r=2 * DH1)
                                 ).then_inc(spread_k[s], 16)

            def spread_queries(body, step):
                s, b = step[1], body.b
                for a in range(2):
                    sp.wait_ge(q_split[s], count(b, 2, a + 1))
                    sp.dma_start(q_parts[a].rearrange("(d p) t -> p d t", p=P), q_hl[:, a, :, :]
                                 ).then_inc(q_saved[s][a], 16)
                if s == "B":
                    spread_keys(body, step)
                for block in range(4):
                    if block % 2 == 0:
                        sp.wait_ge(q_saved[s][block // 2], count(b, 16, 16))
                    for e in range(2):
                        rows = slice(32 * block + DH1 * e, 32 * block + DH1 * (e + 1))
                        src = q_parts[block // 2].rearrange("(p e r) t -> e r p t", e=2, r=DH1)
                        sp.dma_start(q4[rows, e:HEADS:2, :].bitcast(F32), src[e]).then_inc(spread_q[s], 16)

            sp.dma_start(x_tok[:, :, :], x_d[:, 0]).then_inc(x_in, 16)
            sp.dma_start(c_tok[:, :, :], c_d[:, 0]).then_inc(x_in, 16)
            for w, n in ((wq0, "q0"), (wk0, "k0"), (wv0, "v0")):
                sp.dma_start(w[:, :, :], wide(L0 + "W" + n[0])).then_inc(w_in[n], 16)
                if n == "q0":
                    sp.dma_start(mask_u8[:, :, :], m_d[:, 0]).then_inc(m_in, 16)
            sp.dma_start(h_t[:, 0:TT, :].bitcast(I32), io["mask_SxS_ik1"].rearrange("(t p) k -> p t k", p=P)
                         ).then_inc(w_in["mask"], 16)
            sp.dma_start(wo0[:, :, :], wide(L0 + "Wo")).then_inc(w_in["out0"], 16)
            for n in w1:
                sp.dma_start(w1[n][:, :, :], wide(f"{L1}{n}_w")).then_inc(w_in["attn1"], 16)
            for n, src in (("g0", L0 + "gamma"), ("b0", L0 + "beta"), ("g1", L1 + "ln1_g"),
                           ("b1", L1 + "ln1_b"), ("g2", L1 + "ln2_g"), ("b2", L1 + "ln2_b")):
                sp.dma_start(col[n][:, :], column(src), allow_slow_non_contiguous=True
                             ).then_inc(w_in["small"], 16)
            for n, src in (("q", "q_b"), ("k", "k_b"), ("cq", "cq_b"), ("ck", "ck_b"), ("l1", "lin1_b")):
                sp.dma_start(col[n][:, :], column(L1 + src), allow_slow_non_contiguous=True
                             ).then_inc(w_in["small"], 16)
            for n, src in (("bo0", L0 + "bo"), ("g0", L0 + "gamma"), ("b0", L0 + "beta"),
                           ("g1", L1 + "ln1_g"),
                           ("b1", L1 + "ln1_b"), ("g2", L1 + "ln2_g"), ("b2", L1 + "ln2_b"),
                           ("g3", L1 + "ln3_g"), ("b3", L1 + "ln3_b")):
                sp.dma_start(row[n][:, :], io[src].partition_broadcast(P)).then_inc(w_in["small"], 16)
            for n, src in (("o", L1 + "o_b"), ("co", L1 + "co_b"), ("l2", L1 + "lin2_b")):
                sp.dma_start(landing[n], io[src].partition_broadcast(P)).then_inc(w_in["small"], 16)
            for n in w1o:
                src = io[f"{L1}{n}_w"].rearrange("(o f j d) n -> f j d o n", o=DT, f=2, d=DH1)
                for f in range(2):
                    for j in range(4):
                        r = j * SLOT + f * DH1
                        sp.dma_start(w1o[n][r:r + DH1, :, :], src[f, j]).then_inc(w_in["rows1"], 16)
            for n in ("v", "cv"):
                src = io[f"{L1}{n}_b"].rearrange("(o f j d) -> f j d o", o=DT, f=2, d=DH1)
                for f in range(2):
                    for j in range(4):
                        r = j * SLOT + f * DH1
                        sp.dma_start(col[n][r:r + DH1, :], src[f, j], allow_slow_non_contiguous=True
                                     ).then_inc(w_in["rows1"], 16)
            sp.dma_start(wl1[:, :, :], wide(L1 + "lin1_w")).then_inc(w_in["mlp"], 16)
            sp.dma_start(wl2[:, :, :], wide(L1 + "lin2_w")).then_inc(w_in["mlp"], 16)
            sp.wait_ge(zeros_ready, 3)
            for body in bodies(sp, peel_last=True):
                for step in body.steps:
                    if step[:2] == ("IO", "load"):
                        load(body, step)
                    elif step[:2] == ("IO", "store"):
                        store(body, step)
                    elif step[0] == "DMA":
                        {"save": save_keys, "k": spread_keys, "q": spread_queries}[step[2]](body, step)
            sp.wait_ge(out_done, 16 * BATCH + 16)

        @block.tensor
        def _(pe):
            def wait_bank_free(body, step):
                last = body.earlier(step, 2 if step[1] in DVE_JOBS else 1, ring[step[1]])
                if last:
                    (_, name, i), b = last
                    pe.wait_ge(taken[name], count(b, jobs_of(name), i + 1))

            def product(out, lhs, rhs):
                n = len(lhs)
                for i in range(n):
                    last = nc.tensor.matmul(out, lhs[i], rhs[i], start=i == 0, stop=i == n - 1)
                return last

            def transposes(ps, src):
                for d in range(DT):
                    for t in range(TT):
                        last = nc.tensor.transpose(ps[:, d, t * P:(t + 1) * P],
                                                   src[:, t, d * P:(d + 1) * P], ident[:, :])
                return last

            def columns_out(ps, w, first, src):
                for m in range(2):
                    c = (first + m) * P
                    last = product(ps[:, m, :], [w[:, d, c:c + P] for d in range(DT)],
                                   [src[:, d, :] for d in range(DT)])
                return last

            def tokens_out(ps, src, w):
                n = src.shape[1]
                for t in range(TT):
                    last = product(ps[:, t, :], [src[:, d, t * P:(t + 1) * P] for d in range(n)],
                                   [w[:, d, :] for d in range(n)])
                return last

            def job(body, step):
                _, name, i = step
                b = body.batch(name)
                first = body.before is None
                ps = two(bank_of(body, step))
                wait_bank_free(body, step)
                if name == "xT":
                    pe.wait_ge(x_in, count(b, 32, 32))
                    last = transposes(ps, x_tok)
                elif name == "cT":
                    last = transposes(ps, c_tok)
                elif name in ("q", "k"):
                    pe.wait_ge(taken["xT" if name == "q" else "cT"], count(b, 1, 1))
                    if first:
                        pe.wait_ge(w_in[name + "0"], 16)
                    last = columns_out(ps, wq0 if name == "q" else wk0, 2 * i, x_t if name == "q" else c_t)
                elif name == "v":
                    pe.wait_ge(taken["cT"], count(b, 1, 1))
                    if first:
                        pe.wait_ge(w_in["v0"], 16)
                    last = tokens_out(ps, c_t, wv0[:, :, i * D:(i + 1) * D])
                elif name == "kc":
                    if first:
                        pe.wait_ge(w_in["attn1"], 16 * len(w1))
                    last = columns_out(ps, w1["ck"], 0, c_t)
                elif name == "vc":
                    if first:
                        pe.wait_ge(w_in["attn1"], 16 * len(w1))
                    last = tokens_out(ps, c_t, w1["cv"])
                elif name == "wo":
                    pe.wait_ge(ctx_out["A"], count(b, QUADS, QUADS))
                    if first:
                        pe.wait_ge(w_in["out0"], 16)
                    last = tokens_out(ps, k0_ctx, wo0)
                elif name == "x1T":
                    pe.wait_ge(ln_dve["ln0"], count(b, 3, 3))
                    last = transposes(ps, y_a)
                elif name in ("x2T", "x3T"):
                    pe.wait_ge(ln_dve["ln1" if name == "x2T" else "ln2"], count(b, 3, 3))
                    last = transposes(ps, y_b)
                elif name in ("qs", "ks", "qc"):
                    pe.wait_ge(taken["x2T" if name == "qc" else "x1T"], count(b, 1, 1))
                    last = columns_out(ps, w1[{"qs": "q", "ks": "k", "qc": "cq"}[name]], 0, xb_t)
                elif name == "vs":
                    last = tokens_out(ps, xb_t, w1["v"])
                elif name in ("os", "oc"):
                    s = "B" if name == "os" else "C"
                    pe.wait_ge(ctx_out[s], count(b, DT, DT))
                    pe.wait_ge(w_in["rows1"], 16 * 32)
                    last = tokens_out(ps, ctx1, w1o["o" if name == "os" else "co"])
                elif name in ("h", "hd"):
                    pe.wait_ge(taken["x3T"], count(b, 1, 1))
                    pe.wait_ge(w_in["mlp"], 32)
                    last = columns_out(ps, wl1, FF // P - 2 if name == "hd" else 2 * i, x_mlp_t)
                elif name == "y":
                    pe.wait_ge(taken["h"], count(b, 3, 3))
                    pe.wait_ge(taken["hd"], count(b, 1, 1))
                    last = tokens_out(ps, h_t, wl2)
                last.then_inc(filled[name], 1)

            def scores(body, step):
                _, s, p = step
                b = body.batch(s)
                if s == "A":
                    pe.wait_ge(taken["q"], count(b, 4, p // 2 + 1))
                    pe.wait_ge(taken["k"], count(b, 4, p // 2 + 1))
                else:
                    pe.wait_ge(spread_k[s], count(b, 16 * SPREAD["k"], 16 * SPREAD["k"]))
                    pe.wait_ge(spread_q[s], count(b, 16 * SPREAD["q"], 16 * SPREAD["q"]))
                last_pair = body.earlier(step, 1, lambda x: x[0] == "S")
                for e in range(2):
                    if last_pair:
                        (_, s0, p0), b0 = last_pair
                        pe.wait_ge(masked[s0], count(b0, HEADS, 2 * p0 + e + 1))
                    h = 2 * p + e
                    if s == "A":
                        q, k = qz0[:, h % (4 * Q0_RING), :], k0_ctx[:, p, :]
                    else:
                        q, k = q4[:, h, :], k4[:, p, :]
                    for t in range(TT):
                        last = nc.tensor.matmul(two(ps_s[e])[:, t, :], q[:, t * P:(t + 1) * P], k,
                                                start=True, stop=True)
                    last.then_inc(scored[s], 1)

            def turn(body, step):
                _, s, p = step
                b = body.batch(s)
                src = prob[:, body.slot(s, p, P_RING)]
                last_pair = body.earlier(step, 1, lambda x: x[0] == "T")
                for e in range(2):
                    pe.wait_ge(normed[s], count(b, HEADS, 2 * p + e + 1))
                    if last_pair:
                        (_, s0, p0), b0 = last_pair
                        pe.wait_ge((pt_act, pt_dve)[e][s0], count(b0, PAIRS, p0 + 1))
                    for kt in range(TT):
                        for qt in range(TT):
                            last = nc.tensor.transpose(two(ps_t[e])[:, kt, qt * P:(qt + 1) * P],
                                                       src[:, e, qt, kt * P:(kt + 1) * P], ident[:, :])
                    last.then_inc(turned[s], 1)

            def weigh(body, step):
                _, s, quad = step
                b = body.batch(s)
                pe.wait_ge(pt_act[s], count(b, PAIRS, 2 * quad + 2))
                pe.wait_ge(pt_dve[s], count(b, PAIRS, 2 * quad + 2))
                if s == "A":
                    pe.wait_ge(taken["v"], count(b, 4, quad + 1))
                else:
                    pe.wait_ge(taken["vs" if s == "B" else "vc"], count(b, 1, 1))
                last_quad = body.earlier(step, 1, lambda x: x[0] == "AV")
                if last_quad and (s == "A" or quad % 2 == 0):
                    (_, s0, q0), b0 = last_quad
                    pe.wait_ge(ctx_out[s0], count(b0, CTX_OUTS[s0], q0 + 1 if s0 == "A" else q0 // 2 + 1))
                if s == "A":
                    for j in range(2):
                        pt = prob_t[:, body.slot(s, 2 * quad + j, PT_RING)]
                        for kt in range(TT):
                            for e in range(2):
                                h = 4 * quad + 2 * j + e
                                last = nc.tensor.matmul(two(ps_av)[e * DH0:(e + 1) * DH0, j, :],
                                                        v0[:, kt, h * DH0:(h + 1) * DH0], pt[:, e, kt, :],
                                                        start=kt == 0, stop=kt == TT - 1)
                else:
                    for kt in range(TT):
                        for j in range(4):
                            h = 4 * quad + j
                            pt = prob_t[:, body.slot(s, 2 * quad + j // 2, PT_RING)]
                            last = nc.tensor.matmul(ps_av[j * SLOT:(j + 1) * SLOT, 0:TOK],
                                                    v1[s][:, kt, h, :], pt[:, j % 2, kt, :],
                                                    start=kt == 0 and quad % 2 == 0,
                                                    stop=kt == TT - 1 and quad % 2 == 1,
                                                    tile_position=(0, j * SLOT))
                last.then_inc(weighed[s], 1)

            pe.wait_ge(ident_ready, 1)
            for body in bodies(pe):
                for step in body.steps:
                    {"J": job, "S": scores, "T": turn, "AV": weigh}.get(step[0], lambda *_: None)(body, step)

        @block.scalar
        def _(act):
            for n in ("bq", "bk", "bv"):
                act.dma_start(col[n + "0"][:, :], column(L0 + n), allow_slow_non_contiguous=True
                              ).then_inc(w_in["bias0"], 16)
            act.wait_ge(w_in["bias0"], 48)

            def job(body, step):
                _, name, i = step
                b = body.batch(name)
                if name not in ACT_JOBS:
                    return
                ps = two(ps_ga)
                act.wait_ge(filled[name], count(b, jobs_of(name), i + 1))
                if name == "vc":
                    if body.before is None:
                        act.wait_ge(zeros_ready, 2)
                    v = v1["C"][:, :, :, :].rearrange("p t (o f j) d -> p (t o) f j d", f=2, j=4)
                    for f in range(2):
                        last = nc.scalar.activation(
                            v[:, :, f, :, DH1 * f:DH1 * (f + 1)],
                            ps.rearrange("p t (o f j d) -> p (t o) f j d", f=2, j=4, d=DH1)[:, :, f],
                            ACT.Copy)
                    last.then_inc(taken[name], 1)
                    return
                if name in ("x1T", "x2T", "x3T"):
                    n = str(int(name[1]) - 1)
                    for d in range(DT):
                        out = x_mlp_t if name == "x3T" else xb_t
                        last = nc.scalar.activation(out[:, d, :], ps[:, d, :], ACT.Identity,
                                                    bias=col["b" + n][:, d:d + 1],
                                                    scale=col["g" + n][:, d:d + 1])
                    last.then_inc(taken[name], 1)
                    return
                out, bias = (k0_ctx, col["bk0"]) if name == "k" else (h_t, col["l1"])
                for m in range(2):
                    c = 2 * i + m
                    last = nc.scalar.activation(out[:, c, :], ps[:, m, :],
                                                ACT.Relu if name == "h" else ACT.Identity,
                                                bias=bias[:, c:c + 1])
                last.then_inc(taken[name], 1)

            def exps(body, step):
                _, s, p = step
                b = body.batch(s)
                slot = body.slot(s, p, P_RING)
                for e in range(2):
                    act.wait_ge(masked[s], count(b, HEADS, 2 * p + e + 1))
                    for t in range(TT):
                        tile = prob[:, slot, e, t, :]
                        last = nc.scalar.activation(tile, tile, ACT.Exp, bias=ext[:, slot, e, t:t + 1],
                                                    scale=-1.0, accum_out=sums[:, slot, e, t:t + 1])
                    last.then_inc(exped[s], 1)

            def evac_turned(body, step):
                _, s, p = step
                act.wait_ge(turned[s], count(body.batch(s), HEADS, 2 * p + 1))
                nc.scalar.activation(prob_t[:, body.slot(s, p, PT_RING), 0], two(ps_t[0]),
                                     ACT.Copy).then_inc(pt_act[s], 1)

            def evac_weighed(body, step):
                _, s, quad = step
                if s != "A" and quad % 2 == 0:
                    return
                act.wait_ge(weighed[s], count(body.batch(s), QUADS, quad + 1))
                if s == "A":
                    for j in range(2):
                        c = 2 * quad + j
                        last = nc.scalar.activation(k0_ctx[:, c, :], two(ps_av)[:, j, :], ACT.Identity,
                                                    bias=col["bv0"][:, c:c + 1])
                    last.then_inc(ctx_out[s], 1)
                else:
                    act.wait_ge(w_in["rows1"], 16 * 32)
                    o = quad // 2
                    bias = col["v" if s == "B" else "cv"][:, o:o + 1]
                    nc.scalar.activation(ctx1[:, o, :], ps_av[:, 0:TOK], ACT.Identity, bias=bias
                                         ).then_inc(ctx_out[s], 1)

            for body in bodies(act):
                for step in body.steps:
                    {"J": job, "S": exps, "T": evac_turned, "AV": evac_weighed}.get(
                        step[0], lambda *_: None)(body, step)
                if body.before is None:
                    act.wait_ge(w_in["small"], 16 * small)

        @block.vector
        def _(dve):
            nc.vector.memset(qz0[DH0:P, 0:4 * Q0_RING:2, :], 0.0)
            nc.vector.memset(qz0[0:DH0, 1:4 * Q0_RING:2, :], 0.0)
            nc.vector.memset(eps[:, :], EPS)
            nc.vector.memset(minus_half[:, :], -0.5)
            nc.vector.memset(zero[:, :], 0.0).then_inc(out_done, 16)
            dve.wait_ge(out_done, 16)
            nc.vector.memset(mv["a"][:, :, :], 0.0).then_inc(dve_const, 1)
            dve.wait_ge(w_in["bias0"], 48)

            def constants_of_layer1():
                dve.wait_ge(w_in["small"], 16 * small)
                for n, bias in (("b0", "o"), ("b1", "co"), ("b2", "l2")):
                    last = nc.vector.tensor_tensor(row[n][:, :], row[n][:, :], landing[bias], ALU.add)
                last.then_inc(dve_const, 1)
                dve.wait_ge(w_in["mask"], 16)
                nc.vector.tensor_scalar(mask_b[:, :, :], h_t[:, 0:TT, :].bitcast(I32), 0.0, -BIG,
                                        ALU.not_equal, ALU.mult).then_inc(mask_b_ready, 1)
                dve.wait_ge(mask_b_ready, 1)
                dve.wait_ge(zeros_ready, 1)

            def held(value):
                return value if isinstance(value, int) else dve.to_reg(value)

            def job(body, step):
                _, name, i = step
                b = body.batch(name)
                if name == "cT":
                    dve.wait_ge(m_in, count(b, 16, 16))
                    nc.vector.tensor_scalar(mask_a[:, :, :], mask_u8[:, :, :], 0.0, -BIG,
                                            ALU.not_equal, ALU.mult).then_inc(mask_read, 1)
                if name not in DVE_JOBS:
                    return
                bank = bank_of(body, step)
                ps = two(bank)
                dve.wait_ge(filled[name], count(b, jobs_of(name), i + 1))
                if name in ("xT", "cT"):
                    nc.vector.tensor_copy((x_t if name == "xT" else c_t)[:, :, :], ps).then_inc(taken[name], 1)
                elif name == "q":
                    for e in range(2):
                        r = slice(e * DH0, (e + 1) * DH0)
                        first = 4 * (i % Q0_RING) + e
                        bias = col["bq0"][r, 2 * i:2 * i + 2].unsqueeze(2).to_broadcast([DH0, 2, TOK])
                        last = nc.vector.tensor_tensor(qz0[r, first:first + 3:2, :], ps[r], bias, ALU.add)
                    last.then_inc(taken[name], 1)
                elif name == "v":
                    nc.vector.tensor_copy(v0[:, :, i * D:(i + 1) * D], ps).then_inc(taken[name], 1)
                elif name == "vs":
                    v = v1["B"][:, :, :, :].rearrange("p t (o f j) d -> p (t o) f j d", f=2, j=4)
                    for f in range(2):
                        last = nc.vector.tensor_copy(
                            v[:, :, f, :, DH1 * f:DH1 * (f + 1)],
                            ps.rearrange("p t (o f j d) -> p (t o) f j d", f=2, j=4, d=DH1)[:, :, f])
                    last.then_inc(taken[name], 1)
                elif name in ("qs", "qc", "ks", "kc"):
                    s = "B" if name[1] == "s" else "C"
                    if body.before is None:
                        dve.wait_ge(w_in["small"], 16 * small)
                    bias = col[{"qs": "q", "qc": "cq", "ks": "k", "kc": "ck"}[name]]
                    parts, done = (q_hl, q_split[s]) if name[0] == "q" else (k_hl, k_split[s])
                    if name == "qs":
                        dve.wait_ge(k_split["B"], count(b, 2, 2))
                    elif name == "ks":
                        dve.wait_ge(k_split["C"], count(b, 2, 2))
                    elif name == "qc":
                        dve.wait_ge(q_split["B"], count(b, 2, 2))
                    elif body.b is not None:
                        dve.wait_ge(q_split["C"], count(body.b, 2, 2))
                    nc.vector.tensor_tensor(qk[:, :, :], ps, bias[:, :].unsqueeze(2).to_broadcast([P, DT, TOK]),
                                            ALU.add).then_inc(taken[name], 1)
                    if name == "ks":
                        dve.wait_ge(k_saved["C"], count(b, 16, 16))
                    elif name == "kc" and body.b is not None:
                        dve.wait_ge(k_saved["B"], count(body.b, 16, 16))
                    dve.wait_ge(taken[name], count(b, 1, 1))
                    nc.vector.tensor_copy(parts[:, 0].bitcast(F32R), qk[:, :, :]).then_inc(done, 1)
                    dve.wait_ge(done, count(b, 2, 1))
                    nc.vector.tensor_tensor(parts[:, 1].bitcast(F32R), qk[:, :, :], parts[:, 0],
                                            ALU.subtract).then_inc(done, 1)
                elif name == "hd":
                    for m in range(2):
                        c = FF // P - 2 + m
                        last = nc.vector.tensor_scalar(h_t[:, c, :], ps[:, m, :], col["l1"][:, c:c + 1],
                                                       0.0, ALU.add, ALU.max)
                    last.then_inc(taken[name], 1)
                else:
                    residual(name, b, ps)

            def residual(name, b, ps):
                ln = LN_AFTER[name]
                k, y, res = LN_BUFFERS[ln]
                before = {"ln0": "x", "ln1": "ln0", "ln2": "ln1", "ln3": "ln2"}[ln]
                n = 1 if before == "x" else 2
                dve.wait_ge(res_ready[before], count(b, n, n))
                if ln == "ln3":
                    dve.wait_ge(out_done, count(b, 16, 16))
                nc.vector.tensor_tensor(y[:, :, :], ps, res[:, :, :], ALU.add).then_inc(taken[name], 1)
                dve.wait_ge(taken[name], count(b, 1, 1))
                for t in range(TT):
                    last = nc.vector.bn_stats(stats[k][:, t, :], y[:, t, :])
                last.then_inc(ln_dve[ln], 1)
                value = held(count(b, LN_STEPS[ln], 1))
                dve.wait_ge(dve_const, 1)
                dve.wait_ge(ln_dve[ln], value)
                for t in range(TT):
                    last = nc.vector.bn_aggr(mv[k][:, t, :], stats[k][:, t, :])
                last.then_inc(ln_dve[ln], 1)

            def layer_norm(body, step):
                ln = step[1]
                b = body.batch(ln)
                k, y, _ = LN_BUFFERS[ln]
                dve.wait_ge(ln_rstd[ln], count(b, 2, 2))
                for t in range(TT):
                    last = nc.vector.tensor_scalar(y[:, t, :], y[:, t, :], mv[k][:, t, 0:1],
                                                   rstd[k][:, t:t + 1], ALU.subtract, ALU.mult)
                last.then_inc(ln_dve[ln], 1)
                if ln != "ln3":
                    return
                g, beta = (row[n][:, :].unsqueeze(1).to_broadcast([P, TT, D]) for n in LN_ROWS[ln])
                dve.wait_ge(ln_dve[ln], count(b, 5, 3))
                nc.vector.tensor_tensor(y[:, :, :], y[:, :, :], g, ALU.mult).then_inc(ln_dve[ln], 1)
                dve.wait_ge(ln_dve[ln], count(b, 5, 4))
                nc.vector.tensor_tensor(y[:, :, :], y[:, :, :], beta, ALU.add).then_inc(ln_dve[ln], 1)

            def extremes(body, step):
                _, s, p = step
                b = body.batch(s)
                slot = body.slot(s, p, P_RING)
                if s == "A" and p == 0:
                    dve.wait_ge(mask_read, count(b, 1, 1))
                for e in range(2):
                    value = held(count(b, HEADS, 2 * p + e + 1))
                    dve.wait_ge(dve_const, 1)
                    dve.wait_ge(scored[s], value)
                    for t in range(TT):
                        mask = {"A": mask_a[:, t, :], "B": mask_b[:, t, :],
                                "C": zero[:, :].to_broadcast([P, TOK])}[s]
                        last = nc.vector.tensor_tensor_reduce(
                            out=prob[:, slot, e, t, :], in0=two(ps_s[e])[:, t, :], in1=mask,
                            scale=-SCALE[s], scalar=BIG, op0=ALU.add, op1=ALU.min,
                            accum_out=ext[:, slot, e, t:t + 1])
                    last.then_inc(masked[s], 1)

            def reciprocals(body, step):
                _, s, p = step
                slot = body.slot(s, p, P_RING)
                for e in range(2):
                    dve.wait_ge(exped[s], count(body.batch(s), HEADS, 2 * p + e + 1))
                    nc.vector.reciprocal(recip[:, slot, e], sums[:, slot, e]).then_inc(recipd[s], 1)

            def evac_turned(body, step):
                _, s, p = step
                dve.wait_ge(turned[s], count(body.batch(s), HEADS, 2 * p + 2))
                nc.vector.tensor_copy(prob_t[:, body.slot(s, p, PT_RING), 1], two(ps_t[1])).then_inc(pt_dve[s], 1)

            for body in bodies(dve):
                for step in body.steps:
                    {"J": job, "LN": layer_norm, "S": extremes, "R": reciprocals, "T": evac_turned}.get(
                        step[0], lambda *_: None)(body, step)
                if body.before is None:
                    constants_of_layer1()

        @block.gpsimd
        def _(pool):
            nc.gpsimd.memset(ident[:, :], 1.0).then_inc(pool_step, 1)
            pool.wait_ge(pool_step, 1)
            nc.gpsimd.affine_select(out=ident[:, :], in_=ident[:, :], compare_op=ALU.is_equal, fill=0.0,
                                    base=0, pattern=[[-1, P]], channel_multiplier=1).then_inc(ident_ready, 1)
            nc.gpsimd.memset(v1["B"][:, :, :, :], 0.0).then_inc(zeros_ready, 1)
            pool.wait_ge(zeros_ready, 1)
            nc.gpsimd.memset(v1["C"][:, :, :, :], 0.0).then_inc(zeros_ready, 1)
            pool.wait_ge(zeros_ready, 2)
            nc.gpsimd.memset(q4[:, :, :].bitcast(F32), 0.0).then_inc(zeros_ready, 1)
            pool.wait_ge(zeros_ready, 3)
            pool.wait_ge(w_in["small"], 16 * small)
            pool.wait_ge(dve_const, 1)

            def job(body, step):
                _, name, i = step
                b = body.batch(name)
                if name == "xT":
                    pool.wait_ge(x_in, count(b, 32, 32))
                    nc.gpsimd.tensor_tensor(res_a[:, :, :], x_tok[:, :, :],
                                            row["bo0"][:, :].unsqueeze(1).to_broadcast([P, TT, D]),
                                            ALU.add).then_inc(res_ready["x"], 1)
                elif name in LN_AFTER:
                    ln = LN_AFTER[name]
                    k = LN_BUFFERS[ln][0]
                    pool.wait_ge(ln_dve[ln], count(b, LN_STEPS[ln], 2))
                    nc.gpsimd.tensor_tensor(var_eps[k][:, :], mv[k][:, :, 1], eps[:, :],
                                            ALU.add).then_inc(ln_rstd[ln], 1)
                    pool.wait_ge(ln_rstd[ln], count(b, 2, 1))
                    nc.gpsimd.tensor_tensor(rstd[k][:, :], var_eps[k][:, :], minus_half[:, :],
                                            ALU.pow).then_inc(ln_rstd[ln], 1)

            def next_residual(body, step):
                ln = step[1]
                if ln == "ln3":
                    return
                b = body.batch(ln)
                y, out = {"ln0": (y_a, res_ab), "ln1": (y_b, res_b), "ln2": (y_b, res_m)}[ln]
                g, beta = (row[n][:, :].unsqueeze(1).to_broadcast([P, TT, D]) for n in LN_ROWS[ln])
                pool.wait_ge(ln_dve[ln], count(b, 3, 3))
                nc.gpsimd.tensor_tensor(out[:, :, :], y[:, :, :], g, ALU.mult).then_inc(res_ready[ln], 1)
                pool.wait_ge(res_ready[ln], count(b, 2, 1))
                nc.gpsimd.tensor_tensor(out[:, :, :], out[:, :, :], beta, ALU.add).then_inc(res_ready[ln], 1)

            def normalize(body, step):
                _, s, p = step
                slot = body.slot(s, p, P_RING)
                for e in range(2):
                    pool.wait_ge(recipd[s], count(body.batch(s), HEADS, 2 * p + e + 1))
                    rows = prob[:, slot, e]
                    nc.gpsimd.tensor_tensor(rows, rows, recip[:, slot, e].unsqueeze(2)
                                            .to_broadcast([P, TT, TOK]), ALU.mult).then_inc(normed[s], 1)

            for body in bodies(pool):
                for step in body.steps:
                    {"J": job, "LN": next_residual, "R": normalize}.get(
                        step[0], lambda *_: None)(body, step)
                if body.before is None:
                    pool.wait_ge(dve_const, 2)


_OUT = (BATCH, TOK, D)


def kernel(**inputs):
    import concourse.bacc as bacc
    from concourse.bass_utils import run_bass_kernel_spmd

    nc = bacc.Bacc("TRN2", target_bir_lowering=False, num_devices=1)
    arrays = {n: np.ascontiguousarray(a) for n, a in inputs.items()}
    io = {n: nc.dram_tensor(n, a.shape, mybir.dt.from_np(a.dtype), kind="ExternalInput").ap()
          for n, a in arrays.items()}
    io["out"] = nc.dram_tensor("out", _OUT, F32, kind="ExternalOutput").ap()
    program(nc, io)
    return run_bass_kernel_spmd(nc, [arrays], core_ids=[0]).results[0]["out"]
```
